# Optimizing a Trainium2 kernel written in Bass

```python
import numpy as np
import jax
import jax.numpy as jnp

def _softmax(x, axis=-1):
    return jax.nn.softmax(x, axis=axis)

def _gelu(x):
    return jax.nn.gelu(x, approximate=True)

def _silu(x):
    return jax.nn.silu(x)

def _sigmoid(x):
    return jax.nn.sigmoid(x)

def _layernorm(x, axis=-1, eps=1e-05):
    m = jnp.mean(x, axis=axis, keepdims=True)
    v = jnp.var(x, axis=axis, keepdims=True)
    return (x - m) / jnp.sqrt(v + eps)

def _scatter_add(tgt, idx, src, axis=0):
    return tgt.at[idx].add(src)

def _segment_sum(src, seg, n):
    return jax.ops.segment_sum(src, seg, n)
kernel_name = 'mk_sandwich_d2_jaxref_r8_3f8e07'

def setup_inputs(seed: int=0):
    np.random.seed(seed)
    _w = jnp.asarray

    def _L0_attn_setup():
        import jax, jax.numpy as jnp
        import numpy as np
        D_MODEL = 128
        NUM_HEADS = 16
        HEAD_DIM = D_MODEL // NUM_HEADS
        SCALE = HEAD_DIM ** (-0.5)
        key = jax.random.key(seed)
        k1, k2, k3, k4 = jax.random.split(key, 4)
        B, N = (4, 256)
        x = jax.random.normal(k1, (B, N, D_MODEL), dtype=jnp.float32)
        w_qkv = jax.random.normal(k2, (3 * D_MODEL, D_MODEL), dtype=jnp.float32) * D_MODEL ** (-0.5)
        w_proj = jax.random.normal(k3, (D_MODEL, D_MODEL), dtype=jnp.float32) * D_MODEL ** (-0.5)
        b_proj = jax.random.normal(k4, (D_MODEL,), dtype=jnp.float32) * 0.02
        return {'x': x, 'w_qkv': w_qkv, 'w_proj': w_proj, 'b_proj': b_proj}
    _L0_attn_in = _L0_attn_setup()

    def _L0_ffn_setup():
        import jax, jax.numpy as jnp
        import numpy as np
        B, S, H, E = (2, 1024, 128, 8)
        SCALE = 0.5
        key = jax.random.key(seed)
        k1, k2 = jax.random.split(key)
        x = jax.random.normal(k1, (B, S, H), dtype=jnp.float32)
        gate_w = jax.random.normal(k2, (E, H), dtype=jnp.float32) * 0.02
        coeff = SCALE * (1.0 + 0.05 * jnp.arange(E, dtype=jnp.float32))
        expert_w = coeff[:, None, None] * jnp.eye(H, dtype=jnp.float32)
        return {'x': x, 'gate_w': gate_w, 'expert_w': expert_w}
    _L0_ffn_in = _L0_ffn_setup()

    def _L1_attn_setup():
        import jax, jax.numpy as jnp
        import numpy as np
        B, S, IN_DIM, D_MODEL, NUM_HEADS = (4, 256, 128, 128, 16)
        HEAD_DIM = D_MODEL // NUM_HEADS
        CAUSAL = True
        NEG = -9000000000000000.0

        def _xavier(key, shape):
            fan_out, fan_in = shape
            limit = (6.0 / (fan_in + fan_out)) ** 0.5
            return jax.random.uniform(key, shape, jnp.float32, -limit, limit)
        key = jax.random.key(seed)
        ks = jax.random.split(key, 5)
        x = jax.random.normal(ks[0], (B, S, IN_DIM), jnp.float32)
        Wq = _xavier(ks[1], (D_MODEL, IN_DIM))
        Wk = _xavier(ks[2], (D_MODEL, IN_DIM))
        Wv = _xavier(ks[3], (D_MODEL, IN_DIM))
        Wo = _xavier(ks[4], (D_MODEL, D_MODEL))
        bq = jnp.zeros((D_MODEL,), jnp.float32)
        bk = jnp.zeros((D_MODEL,), jnp.float32)
        bv = jnp.zeros((D_MODEL,), jnp.float32)
        bo = jnp.zeros((D_MODEL,), jnp.float32)
        return {'x': x, 'Wq': Wq, 'bq': bq, 'Wk': Wk, 'bk': bk, 'Wv': Wv, 'bv': bv, 'Wo': Wo, 'bo': bo}
    _L1_attn_in = _L1_attn_setup()

    def _L1_ffn_setup():
        import jax, jax.numpy as jnp
        import numpy as np
        B, S, H = (2, 128, 128)
        E, F = (8, 512)
        GATE_TEMP = 0.1
        key = jax.random.key(seed)
        ks = jax.random.split(key, 6)
        s_h = 1.0 / np.sqrt(H)
        s_f = 1.0 / np.sqrt(F)
        return {'hidden_states': jax.random.normal(ks[0], (B, S, H), dtype=jnp.float32), 'w_router': jax.random.normal(ks[1], (H, E), dtype=jnp.float32) * s_h, 'w_gating': jax.random.normal(ks[2], (H, E), dtype=jnp.float32) * s_h, 'w_gate': jax.random.normal(ks[3], (E, H, F), dtype=jnp.float32) * s_h, 'w_up': jax.random.normal(ks[4], (E, H, F), dtype=jnp.float32) * s_h, 'w_down': jax.random.normal(ks[5], (E, F, H), dtype=jnp.float32) * s_f}
    _L1_ffn_in = _L1_ffn_setup()
    _d = {'L0_attn_x': _L0_attn_in['x'], 'L0_attn_w_qkv': _L0_attn_in['w_qkv'], 'L0_attn_w_proj': _L0_attn_in['w_proj'], 'L0_attn_b_proj': _L0_attn_in['b_proj'], 'L0_ffn_gate_w': _L0_ffn_in['gate_w'], 'L0_ffn_expert_w': _L0_ffn_in['expert_w'], 'L1_attn_Wq': _L1_attn_in['Wq'], 'L1_attn_bq': _L1_attn_in['bq'], 'L1_attn_Wk': _L1_attn_in['Wk'], 'L1_attn_bk': _L1_attn_in['bk'], 'L1_attn_Wv': _L1_attn_in['Wv'], 'L1_attn_bv': _L1_attn_in['bv'], 'L1_attn_Wo': _L1_attn_in['Wo'], 'L1_attn_bo': _L1_attn_in['bo'], 'L1_ffn_w_router': _L1_ffn_in['w_router'], 'L1_ffn_w_gating': _L1_ffn_in['w_gating'], 'L1_ffn_w_gate': _L1_ffn_in['w_gate'], 'L1_ffn_w_up': _L1_ffn_in['w_up'], 'L1_ffn_w_down': _L1_ffn_in['w_down']}
    _x0 = _d['L0_attn_x']
    _d['L0_attn_x'] = jax.random.normal(jax.random.fold_in(jax.random.key(seed), 1), (1, 2048, 128), dtype=_x0.dtype)
    del _x0
    return _d

def reference(L0_attn_x, L0_attn_w_qkv, L0_attn_w_proj, L0_attn_b_proj, L0_ffn_gate_w, L0_ffn_expert_w, L1_attn_Wq, L1_attn_bq, L1_attn_Wk, L1_attn_bk, L1_attn_Wv, L1_attn_bv, L1_attn_Wo, L1_attn_bo, L1_ffn_w_router, L1_ffn_w_gating, L1_ffn_w_gate, L1_ffn_w_up, L1_ffn_w_down):

    def _L0_attn_ref(x, w_qkv, w_proj, b_proj):
        import jax, jax.numpy as jnp
        import numpy as np
        D_MODEL = 128
        NUM_HEADS = 16
        HEAD_DIM = D_MODEL // NUM_HEADS
        SCALE = HEAD_DIM ** (-0.5)
        B, N, C = x.shape
        qkv = jnp.einsum('bnc,dc->bnd', x, w_qkv)
        qkv = qkv.reshape(B, N, 3, NUM_HEADS, HEAD_DIM)
        qkv = jnp.transpose(qkv, (2, 0, 3, 1, 4))
        q, k, v = (qkv[0], qkv[1], qkv[2])
        q = q * SCALE
        attn = jnp.einsum('bhnd,bhmd->bhnm', q, k)
        attn = jax.nn.softmax(attn, axis=-1)
        out = jnp.einsum('bhnm,bhmd->bhnd', attn, v)
        out = jnp.transpose(out, (0, 2, 1, 3)).reshape(B, N, C)
        return jnp.einsum('bnc,dc->bnd', out, w_proj) + b_proj

    def _L0_ffn_ref(x, gate_w, expert_w):
        import jax, jax.numpy as jnp
        import numpy as np
        B, S, H, E = (2, 1024, 128, 8)
        SCALE = 0.5
        scores = jnp.einsum('bsh,eh->bse', x, gate_w)
        chosen = jnp.argmax(scores, axis=-1)
        onehot = jax.nn.one_hot(chosen, gate_w.shape[0], dtype=x.dtype)
        expert_out = jnp.einsum('bsh,efh->bsef', x, expert_w)
        return x + jnp.einsum('bsef,bse->bsf', expert_out, onehot)

    def _L1_attn_ref(x, Wq, bq, Wk, bk, Wv, bv, Wo, bo):
        import jax, jax.numpy as jnp
        import numpy as np
        B, S, IN_DIM, D_MODEL, NUM_HEADS = (4, 256, 128, 128, 16)
        HEAD_DIM = D_MODEL // NUM_HEADS
        CAUSAL = True
        NEG = -9000000000000000.0

        def _xavier(key, shape):
            fan_out, fan_in = shape
            limit = (6.0 / (fan_in + fan_out)) ** 0.5
            return jax.random.uniform(key, shape, jnp.float32, -limit, limit)
        batch, seq, _ = x.shape
        q = x @ Wq.T + bq
        k = x @ Wk.T + bk
        v = x @ Wv.T + bv

        def split(t):
            return t.reshape(batch, seq, NUM_HEADS, HEAD_DIM).transpose(0, 2, 1, 3)
        q, k, v = (split(q), split(k), split(v))
        scores = jnp.einsum('bhqd,bhkd->bhqk', q, k) / jnp.sqrt(jnp.float32(HEAD_DIM))
        if CAUSAL:
            mask = jnp.tril(jnp.ones((seq, seq), bool))
            scores = jnp.where(mask, scores, jnp.float32(NEG))
        attn = jax.nn.softmax(scores, axis=-1)
        out = jnp.einsum('bhqk,bhkd->bhqd', attn, v)
        out = out.transpose(0, 2, 1, 3).reshape(batch, seq, D_MODEL)
        return out @ Wo.T + bo

    def _L1_ffn_ref(hidden_states, w_router, w_gating, w_gate, w_up, w_down):
        import jax, jax.numpy as jnp
        import numpy as np
        B, S, H = (2, 128, 128)
        E, F = (8, 512)
        GATE_TEMP = 0.1
        x = hidden_states
        router_probs = jax.nn.softmax(jnp.einsum('bsh,he->bse', x, w_router), axis=-1)
        gate_weights = jax.nn.softmax(jnp.einsum('bsh,he->bse', x, w_gating) / GATE_TEMP, axis=-1)
        g = jnp.einsum('bsh,ehf->ebsf', x, w_gate)
        u = jnp.einsum('bsh,ehf->ebsf', x, w_up)
        h = jax.nn.silu(g) * u
        expert_out = jnp.einsum('ebsf,efh->ebsh', h, w_down)
        cw = router_probs * gate_weights
        cw = cw / (jnp.sum(cw, axis=-1, keepdims=True) + 1e-09)
        out = jnp.einsum('ebsh,bse->bsh', expert_out, cw)
        return out
    x = L0_attn_x
    x = x + _layernorm(_L0_attn_ref(_layernorm(x, axis=-1), L0_attn_w_qkv, L0_attn_w_proj, L0_attn_b_proj), axis=-1)
    x = x + _layernorm(_L0_ffn_ref(_layernorm(x, axis=-1), L0_ffn_gate_w, L0_ffn_expert_w), axis=-1)
    x = x + _layernorm(_L1_attn_ref(_layernorm(x, axis=-1), L1_attn_Wq, L1_attn_bq, L1_attn_Wk, L1_attn_bk, L1_attn_Wv, L1_attn_bv, L1_attn_Wo, L1_attn_bo), axis=-1)
    x = x + _layernorm(_L1_ffn_ref(_layernorm(x, axis=-1), L1_ffn_w_router, L1_ffn_w_gating, L1_ffn_w_gate, L1_ffn_w_up, L1_ffn_w_down), axis=-1)
    return x

_drawn_inputs = setup_inputs


def setup_inputs(seed=0):
    import zlib

    import numpy as np

    out = dict(_drawn_inputs(seed))
    spreads = {'L1_attn_bq': (0.0, 0.1),
     'L1_attn_bk': (0.0, 0.1),
     'L1_attn_bv': (0.0, 0.1),
     'L1_attn_bo': (0.0, 0.1)}
    factors = {}
    for name, (base, spread) in spreads.items():
        noise = np.random.default_rng([zlib.crc32(name.encode()), seed]).standard_normal(out[name].shape)
        drawn = base * np.exp(spread * noise) if base else spread * noise
        out[name] = jnp.asarray(drawn.astype(out[name].dtype))
    for name, factor in factors.items():
        out[name] = (out[name] * factor).astype(out[name].dtype)
    return out
```

```python
import concourse.bass as bass
from concourse import mybir
from contextlib import ExitStack

FP32 = mybir.dt.float32
BF16 = mybir.dt.bfloat16
ALU = mybir.AluOpType
ACT = mybir.ActivationFunctionType
AX = mybir.AxisListType

P = 128
N = 2048
NT = N // P
C = 512
NC = N // C
TC = C // P
H = 16
HD = P // H
SCALE = HD ** -0.5
NE = 8
F = 512
FB = F // P
LN_EPS = 1e-5
MASKED = -9e15
GATE_TEMP = 0.1

PARTS = 3
ROWS = PARTS * PARTS * HD
NAT_ROWS = 96
SHIFT_ROW = 96
T_ROWS = SHIFT_ROW + PARTS


class Chain:

    def __init__(self, sem):
        self.sem, self.n, self.turn, self.per, self.start = sem, 0, None, 0, 0

    def enter(self, turn, per):
        self.turn, self.per, self.start = turn, per, self.n

    def leave(self, turns):
        assert self.n - self.start == self.per, (self.n - self.start, self.per)
        self.n, self.turn = self.start + self.per * turns, None

    def value(self):
        return self.n if self.turn is None else self.turn * self.per + self.n


def sandwich(nc, x_in, w_qkv, w_proj, b_proj, gate_w, expert_w, Wq, bq, Wk, bk, Wv, bv, Wo, bo,
             w_router, w_gating, w_gate, w_up, w_down, out):
    ctx = ExitStack()
    with ctx:
        def sb(name, shape, dt=FP32):
            return ctx.enter_context(nc.sbuf_tensor(name, shape, dt))

        sems = {}

        def sem(name):
            if name not in sems:
                sems[name] = ctx.enter_context(nc.semaphore(name))
            return sems[name]

        X = sb("X", [P, NT, P])
        XN = sb("XN", [P, NT, P])
        XT = sb("XT", [P, N])
        ON = sb("ON", [P, NT, P])
        ident = sb("ident", [P, P])
        identb = sb("identb", [P, P], BF16)
        mask_nat = sb("mask_nat", [P, P], BF16)
        mask_t = sb("mask_t", [P, P], BF16)
        WT = sb("WT", [P, 16, P])
        gateT = sb("gateT", [P, NE])
        rgw = sb("rgw", [P, 2, NE])
        bias_bc = sb("bias_bc", [P, 3, P])
        bias_qk = sb("bias_qk", [P, 2])
        Wg = sb("Wg", [P, NE, F])
        Wu = sb("Wu", [P, NE, F])
        probs = sb("probs", [P, 4, C])
        probs_diag = sb("probs_diag", [P, TC, C])
        o_sb = sb("o_sb", [P, 2, C])
        max_row = sb("max_row", [P, 2, P], BF16)
        stats = sb("stats", [P, TC, 6])
        held = sb("held", [P, 2])
        mv = sb("mv", [P, TC, 2])
        var_eps = sb("var_eps", [P, TC])
        std = sb("std", [P, TC])
        rstd = sb("rstd", [P, TC])
        mx = sb("mx", [P, 2, TC, 2])
        neg_max = sb("neg_max", [P, TC])
        rest1 = sb("rest1", [P, TC])
        rest2 = sb("rest2", [P, TC])
        max_parts = sb("max_parts", [P, 2, PARTS, TC], BF16)
        osum = sb("osum", [P, TC, HD + 1])
        oinv = sb("oinv", [P, TC])
        logit = sb("logit", [P, NT, 2, NE])
        expo = sb("expo", [P, NT, 2, NE])
        lred = sb("lred", [P, NT, 2])
        linv = sb("linv", [P, NT, 2])
        cw = sb("cw", [P, NT, NE])
        cwT = sb("cwT", [P, P])
        tie = sb("tie", [P, TC, NE])
        sc_max = sb("sc_max", [P, TC])
        sc_hit = sb("sc_hit", [P, TC, NE])
        onehot = sb("onehot", [P, TC, NE])

        A = sb("A", [P, 20480])
        V = A[:, 0:2048].rearrange("p (t h d) -> p t h d", t=NT, h=H)
        VH = [A[:, 2048 + 512 * s:2560 + 512 * s].rearrange("p (t d) -> p t d", t=NT)
              for s in range(2)]
        QS = [A[:, 8192 + 1024 * s:8192 + 1024 * (s + 1)].bitcast(BF16) for s in range(2)]
        KS = [A[:, 10240 + 1024 * s:10240 + 1024 * (s + 1)].bitcast(BF16) for s in range(2)]
        QP = A[:, 12288:15360].bitcast(BF16).rearrange("p (a n) -> p a n", a=PARTS)
        KP = A[:, 15360:18432].bitcast(BF16).rearrange("p (a n) -> p a n", a=PARTS)
        QF = [A[:, 18432 + C * i:18432 + C * (i + 1)] for i in range(2)]
        QR = [A[:, 19456 + C * i:19456 + C * (i + 1)] for i in range(2)]
        raw = A[:, 12288:14336].rearrange("p (b c) -> p b c", b=16)
        raw_gate = A[0:NE, 14336:14336 + P]
        picked = A[:, 12288:12288 + NE * P].rearrange("p (e f) -> p e f", e=NE)
        CWB = [A[:, 4096 * i:4096 * (i + 1)].rearrange("p (e n) -> p e n", e=NE) for i in range(2)]
        HB = [A[:, 8192 + C * i:8192 + C * (i + 1)] for i in range(4)]
        SG = [A[:, 10240 + C * i:10240 + C * (i + 1)] for i in range(4)]
        XC = [A[:, 12288 + C * i:12288 + C * (i + 1)] for i in range(2)]
        Wd = A[:, 16384:20480].rearrange("p (k h) -> p k h", h=P)

        W_Q, W_K, W_V, W_O = (0, 4), (1, 5), (2, 6), (3, 7)
        W_E = 8

        PS = ctx.enter_context(nc.psum_tensor("PS", [P, 8 * C], FP32))

        def bank(i, n=1):
            return PS[:, i * C:(i + n) * C]

        QD = [nc.dram_tensor(f"q_parts{l}", (PARTS, P, N), BF16, kind="Internal").ap() for l in range(2)]
        KD = [nc.dram_tensor(f"k_parts{l}", (PARTS, P, N), BF16, kind="Internal").ap() for l in range(2)]
        CD = nc.dram_tensor("cw_rows", (NE, N), FP32, kind="Internal").ap()

        link_sem = sem("dve_link")
        link_chain = Chain(link_sem)
        var_chain, std_chain = Chain(sem("var_ready")), Chain(sem("std_ready"))
        act_norms = [Chain(sem("var_ready")), Chain(sem("std_ready"))]

        def dve_link(dve, ins):
            link_chain.n += 1
            ins.then_inc(link_chain.sem, 1)
            dve.wait_ge(link_chain.sem, link_chain.value())

        def hold_wait():
            nc.vector.tensor_copy(held[:, 1:2], held[:, 0:1])

        def dve_norm(dve, src, ready=None):
            hold_wait()
            for t in range(TC):
                ins = nc.vector.bn_stats(stats[:, t, :], src(t))
            dve_link(dve, ins)
            hold_wait()
            for t in range(TC):
                ins = nc.vector.bn_aggr(mv[:, t, :], stats[:, t, :])
            dve_link(dve, ins)
            var_chain.n += 1
            nc.vector.tensor_scalar(var_eps[:, :], mv[:, :, 1], LN_EPS, None, ALU.add).then_inc(var_chain.sem, 1)
            std_chain.n += 1
            dve.wait_ge(std_chain.sem, std_chain.value())
            dve_link(dve, nc.vector.reciprocal(rstd[:, :], std[:, :]))

        def dve_scale(dst, src, t):
            return nc.vector.tensor_scalar(dst, src, mv[:, t, 0:1], rstd[:, t:t + 1],
                                           ALU.subtract, ALU.mult)

        def act_std(act):
            v, s = act_norms
            v.n += 1
            s.n += 1
            act.wait_ge(v.sem, v.value())
            nc.scalar.activation(std[:, :], var_eps[:, :], ACT.Sqrt).then_inc(s.sem, 1)

        def tile_of(buf, c, t):
            return buf[:, c * TC + t, :]

        def chunk_of(buf, c):
            return buf[:, bass.ds(c * TC, TC), :]

        def cols(c, t=0, n=C):
            return bass.ds(c * C + t * P, n)

        def loop(eng, chains, per, turns=NC):
            class L:
                def __enter__(s):
                    s.f = eng.Fori(0, turns)
                    i = s.f.__enter__()
                    for ch, p in zip(chains, per):
                        ch.enter(i, p)
                    return i

                def __exit__(s, *a):
                    for ch in chains:
                        if a[0] is None:
                            ch.leave(turns)
                    return s.f.__exit__(*a)
            return L()

        def key_tiles(l, c):
            return NT if l == 0 else TC * (c + 1)

        ORDER = [[0, 1, 2, 3], [0, 3, 1, 2]]
        LEAD = 2

        def max_items(l, c):
            items = []
            for t in range(TC):
                n = N if l == 0 else (TC * c + t + 1) * P
                for s, k0 in enumerate(range(0, n, 2 * C)):
                    pieces = []
                    for k in range(k0, min(k0 + 2 * C, n), C):
                        w = min(C, n - k)
                        pieces.append((k, w, l == 1 and k + w == n))
                    items.append((t, s, pieces))
            return items

        SLOTS = [[2, 2, 2, 2], [1, 1, 2, 2]]
        STEPS = [sum(key_tiles(l, c) for c in range(NC)) for l in range(2)]
        ITEMS = [sum(len(max_items(l, c)) for c in range(NC)) for l in range(2)]

        def units(l, pair_first, pair_last):
            order, res, step = ORDER[l], [], 0
            item0 = [0]
            for j in range(2 * NC + LEAD):
                item0.append(item0[-1] + len(max_items(l, order[j % NC])))
            for j in range(2 * NC):
                c = order[j % NC]
                v = j + LEAD
                ahead = None if pair_last and v >= 2 * NC else (v // NC, order[v % NC], item0[v])
                res.append((j, j // NC, c, step, ahead))
                step += key_tiles(l, c)
            return res

        def o_pos(l, c, nitems):
            at = 3
            return at, sum(1 for k in range(nitems) if k * key_tiles(l, c) // max(nitems, 1) < at)

        def m_pos(l, c):
            return 8 if key_tiles(l, c) > 8 else key_tiles(l, c)

        class Turn:

            def __init__(self, l, g):
                self.l, self.g = l, g

            def steps(self, n):
                return self.g * (2 * STEPS[self.l]) + n

            def items(self, n):
                return self.g * (2 * ITEMS[self.l]) + n

            def units(self, n):
                return self.g * (2 * NC) + n

            def heads(self, n):
                return self.g * 2 + n

        def pairs(eng, l, body):
            body(Turn(l, 0), True, False)
            with eng.Fori(1, H // 2 - 1) as g:
                body(Turn(l, g), False, False)
            body(Turn(l, H // 2 - 1), False, True)

        def asem(l, name):
            return sem(f"{name}{l}")

        def pe_max_item(pe, l, T, s, c, r, item):
            t, _, pieces = item
            if not (isinstance(T.g, int) and T.g == 0 and r < 2):
                pe.wait_ge(asem(l, "max_taken"), T.items(r - 1))
            at = (r % 2) * 2
            q = QS[s % 2][0:NAT_ROWS, c * C + t * P:c * C + (t + 1) * P]
            for n, (k, w, diag) in enumerate(pieces):
                dst = PS[:, (at + n) * C:(at + n) * C + w]
                ins = nc.tensor.matmul(dst, q, KS[s % 2][0:NAT_ROWS, k:k + w], start=True, stop=not diag)
                if diag:
                    ins = nc.tensor.matmul(dst[:, w - P:w], identb[:, :], mask_nat[:, :], start=False, stop=True)
            ins.then_inc(asem(l, "max_scores"), 1)

        def pe_max_transpose(pe, l, T, v):
            pe.wait_ge(asem(l, "max_parts_ready"), T.units(v + 1))
            dst = PS[0:PARTS * TC, (6 + v % 2) * C:(6 + v % 2) * C + P // 2].bitcast(BF16)
            nc.tensor.transpose(dst, max_parts[:, v % 2, :, :].rearrange("p a t -> p (a t)"),
                                identb[:, :]).then_inc(asem(l, "max_rows"), 1)

        def pe_attention(pe, l):
            pe.wait_ge(sem(f"v_taken{l}"), NC)
            pe.wait_ge(asem(l, "operands"), OPERANDS)
            T0 = Turn(l, 0)
            r = 0
            for v in range(LEAD):
                for item in max_items(l, ORDER[l][v]):
                    pe_max_item(pe, l, T0, 0, ORDER[l][v], r, item)
                    r += 1
                if v == 0:
                    pe_max_transpose(pe, l, T0, 0)

            def body(T, first, last):
                for j, s, c, step0, ahead in units(l, first, last):
                    nk = key_tiles(l, c)
                    items = max_items(l, ahead[1]) if ahead else []
                    opos, _ = o_pos(l, c, len(items))
                    mpos = m_pos(l, c)
                    has_o = not (first and j == 0)
                    has_m = not (last and j == 2 * NC - 1)
                    ob = (6 + j % 2) * C
                    r = 0

                    def scores(i):
                        n = step0 + i
                        if not (first and n < 2):
                            pe.wait_ge(asem(l, "exp_done"), T.steps(n - 1))
                        if i == 0:
                            pe.wait_ge(asem(l, "max_shift"), T.units(j + 1) * 48)
                        q0 = P * (i - (nk - TC)) if l == 1 and i >= nk - TC else 0
                        dst = PS[:, (4 + n % 2) * C + q0:(5 + n % 2) * C]
                        diag = l == 1 and i >= nk - TC
                        ins = nc.tensor.matmul(dst, KS[s][0:T_ROWS, i * P:(i + 1) * P],
                                               QS[s][0:T_ROWS, c * C + q0:(c + 1) * C], start=True, stop=not diag)
                        if diag:
                            ins = nc.tensor.matmul(dst[:, 0:P], identb[:, :], mask_t[:, :], start=False, stop=True)
                        ins.then_inc(asem(l, "scores_t"), 1)

                    def weigh(i):
                        n = step0 + i
                        pe.wait_ge(asem(l, "exp_done"), T.steps(n + 1))
                        if i == 0 and not (first and j < 2):
                            pe.wait_ge(asem(l, "o_used"), T.units(j - 1))
                        diag = l == 1 and i >= nk - TC
                        q0 = P * (i % TC) if diag and c > 0 else 0
                        src = probs_diag[:, i % TC, q0:C] if diag else probs[:, n % 4, :]
                        g = i % TC
                        nc.tensor.matmul(PS[32 * g:32 * g + 32, ob + q0:ob + C], VH[s][:, i, :], src,
                                         start=i < TC, stop=i >= nk - TC,
                                         skip_group_check=True).then_inc(asem(l, "weighed"), 1)

                    if j % NC == 0:
                        pe.wait_ge(asem(l, "values"), T.heads(s + 1))
                    if j % NC == NC - LEAD and ahead:
                        pe.wait_ge(asem(l, "operands"), T.heads(s + 2) * OPERANDS)
                    for i in range(nk + 2):
                        if i == opos and has_o:
                            pe.wait_ge(asem(l, "o_copied"), T.units(j))
                            for t in range(TC):
                                ins = nc.tensor.transpose(
                                    PS[:, (6 + (j + 1) % 2) * C + t * P:(6 + (j + 1) % 2) * C + (t + 1) * P],
                                    o_sb[:, (j + 1) % 2, t * P:(t + 1) * P], ident[:, :])
                            ins.then_inc(asem(l, "o_transposed"), 1)
                        if i == mpos and has_m:
                            if has_o:
                                pe.wait_ge(asem(l, "o_used"), T.units(j))
                            pe_max_transpose(pe, l, T, j + 1)
                        if i < nk:
                            scores(i)
                            while r < len(items) and r * nk // len(items) <= i:
                                pe_max_item(pe, l, T, ahead[0], ahead[1], ahead[2] + r, items[r])
                                r += 1
                        if i >= 2:
                            weigh(i - 2)

            pairs(pe, l, body)
            pe.wait_ge(asem(l, "o_copied"), H * NC)
            for t in range(TC):
                ins = nc.tensor.transpose(PS[:, 7 * C + t * P:7 * C + (t + 1) * P],
                                          o_sb[:, 1, t * P:(t + 1) * P], ident[:, :])
            ins.then_inc(asem(l, "o_transposed"), 1)

        def act_o_copy(act, l, T, j):
            n = sum(key_tiles(l, ORDER[l][u % NC]) for u in range(j + 1)) if j >= 0 else 0
            act.wait_ge(asem(l, "weighed"), T.steps(n))
            if not (isinstance(T.g, int) and T.g == 0 and j < 2):
                act.wait_ge(asem(l, "o_used"), T.units(j - 1))
            nc.scalar.copy(o_sb[:, j % 2, :], bank(6 + j % 2)).then_inc(asem(l, "o_copied"), 1)

        def act_max_copy(act, l, T, v):
            act.wait_ge(asem(l, "max_rows"), T.units(v + 1))
            if not (isinstance(T.g, int) and T.g == 0 and v < 2):
                act.wait_ge(asem(l, "max_shift"), T.units(v - 1) * 48)
            src = PS[0:PARTS * TC, (6 + v % 2) * C:(6 + v % 2) * C + P // 2].bitcast(BF16)
            nc.scalar.copy(max_row[0:PARTS * TC, v % 2, :], src).then_inc(asem(l, "max_row_copied"), 1)

        def act_attention(act, l):
            act_max_copy(act, l, Turn(l, 0), 0)

            def body(T, first, last):
                for j, s, c, step0, ahead in units(l, first, last):
                    nk = key_tiles(l, c)
                    for i in range(nk):
                        n = step0 + i
                        if i == 2 and not (first and j == 0):
                            act_o_copy(act, l, T, j - 1)
                        if i == m_pos(l, c) and not (last and j == 2 * NC - 1):
                            act_max_copy(act, l, T, j + 1)
                        diag = l == 1 and i >= nk - TC
                        act.wait_ge(asem(l, "scores_t"), T.steps(n + 1))
                        if diag:
                            if not (first and j == 0):
                                act.wait_ge(asem(l, "weighed"), T.steps(step0))
                        elif not (first and n < 4):
                            act.wait_ge(asem(l, "weighed"), T.steps(n - 3))
                        q0 = P * (i % TC) if diag else 0
                        dst = probs_diag[:, i % TC, q0:C] if diag else probs[:, n % 4, :]
                        nc.scalar.activation(dst, PS[:, (4 + n % 2) * C + q0:(5 + n % 2) * C], ACT.Exp,
                                             scale=SCALE).then_inc(asem(l, "exp_done"), 1)
                    if nk == m_pos(l, c) and not (last and j == 2 * NC - 1):
                        act_max_copy(act, l, T, j + 1)

            pairs(act, l, body)
            act_o_copy(act, l, Turn(l, H // 2 - 1), 2 * NC - 1)

        def dve_max_chain(dve, l, T, v):
            c = ORDER[l][v % NC]
            dve_link(dve, nc.vector.tensor_reduce(neg_max[:, :], mx[:, v % 2, :, 0:SLOTS[l][c]], AX.X, ALU.max,
                                                  negate=True))
            if not (isinstance(T.g, int) and T.g == 0 and v < 2):
                dve.wait_ge(asem(l, "max_rows"), T.units(v - 1))
            m = max_parts[:, v % 2]
            dve_link(dve, nc.vector.tensor_copy(m[:, 0, :], neg_max[:, :]))
            dve_link(dve, nc.vector.tensor_tensor(rest1[:, :], neg_max[:, :], m[:, 0, :], ALU.subtract))
            dve_link(dve, nc.vector.tensor_copy(m[:, 1, :], rest1[:, :]))
            nc.vector.tensor_tensor(m[:, 2, :], rest1[:, :], m[:, 1, :], ALU.subtract)\
                .then_inc(asem(l, "max_parts_ready"), 1)

        MAX_LINKS = 4

        def dve_reduce(dve, l, T, v, r, item):
            t, slot, pieces = item
            w = pieces[-1][0] + pieces[-1][1] - pieces[0][0]
            dve.wait_ge(asem(l, "max_scores"), T.items(r + 1))
            at = (r % 2) * 2 * C
            return nc.vector.tensor_reduce(mx[:, v % 2, t, slot:slot + 1], PS[:, at:at + w], AX.X, ALU.max)\
                .then_inc(asem(l, "max_taken"), 1)

        def dve_output(dve, l, T, j, s, c):
            dve.wait_ge(asem(l, "o_transposed"), T.units(j + 1))
            if not (isinstance(T.g, int) and T.g == 0 and j == 0):
                dve.wait_ge(asem(l, "o_used"), T.units(j))
            src = bank(6 + j % 2).rearrange("p (t g d) -> p t d g", t=TC, g=4)
            dve_link(dve, nc.vector.tensor_reduce(osum[:, :, :], src[:, :, 0:HD + 1, :], AX.X, ALU.add))
            dve_link(dve, nc.vector.reciprocal(oinv[:, :], osum[:, :, HD]))
            dst = ON[:, c * TC:(c + 1) * TC, bass.ds(T.heads(s) * HD, HD)]
            nc.vector.tensor_tensor(dst, osum[:, :, 0:HD], oinv[:, :].unsqueeze(2).broadcast_to((P, TC, HD)),
                                    ALU.mult).then_inc(asem(l, "o_used"), 1)

        OUT_LINKS = 2

        def dve_attention(dve, l):
            T0 = Turn(l, 0)
            r = 0
            for v in range(LEAD):
                for item in max_items(l, ORDER[l][v]):
                    dve_reduce(dve, l, T0, v, r, item)
                    r += 1
                dve.wait_ge(asem(l, "max_taken"), r)
                dve_max_chain(dve, l, T0, v)

            def body(T, first, last):
                for j, s, c, step0, ahead in units(l, first, last):
                    items = max_items(l, ahead[1]) if ahead else []
                    _, before = o_pos(l, c, len(items))
                    pj = j - 1
                    for n in range(len(items) + 1):
                        if n == before and not (first and j == 0):
                            dve_output(dve, l, T, pj, pj // NC if pj >= 0 else -1, ORDER[l][pj % NC])
                        if n < len(items):
                            dve_reduce(dve, l, T, j + LEAD, ahead[2] + n, items[n])
                    if ahead:
                        dve.wait_ge(asem(l, "max_taken"), T.items(ahead[2] + len(items)))
                        dve_max_chain(dve, l, T, j + LEAD)

            per = 2 * NC * (MAX_LINKS + OUT_LINKS)
            body(Turn(l, 0), True, False)
            turns = H // 2 - 2
            with dve.Fori(1, H // 2 - 1) as g:
                base = link_chain.n
                link_chain.n -= per
                link_chain.enter(g, per)
                body(Turn(l, g), False, False)
            link_chain.leave(turns + 1)
            assert link_chain.n == base + per * turns
            body(Turn(l, H // 2 - 1), False, True)
            dve_output(dve, l, Turn(l, H // 2 - 1), 2 * NC - 1, 1, ORDER[l][NC - 1])

        def pool_attention(pool, l):
            pool.wait_ge(sem(f"v_taken{l}"), NC)

            def values(T, s, free):
                if free:
                    pool.wait_ge(asem(l, "weighed"), T.steps((s - 1) * STEPS[l]))
                nc.gpsimd.tensor_copy(VH[s % 2][:, :, 0:HD], V[:, :, T.heads(s), :]).then_inc(asem(l, "values"), 1)

            def body(T, first, last):
                for s in range(2):
                    values(T, s, not first)

            pairs(pool, l, body)

        OPERANDS = 2 * PARTS * 16

        def sp_operands(sp, l, head, s):
            for a in range(PARTS):
                rows = slice(a * PARTS * HD, (a + 1) * PARTS * HD)
                q = bass.AP(QD[l].tensor, head * (HD * N) + a * P * N, [[0, PARTS], [N, HD], [1, N]])
                k = bass.AP(KD[l].tensor, head * (HD * N), [[P * N, PARTS], [N, HD], [1, N]])
                sp.dma_start(QS[s][rows, :], q).then_inc(asem(l, "operands"), 16)
                sp.dma_start(KS[s][rows, :], k).then_inc(asem(l, "operands"), 16)

        def sp_max_rows(sp, l, T, v):
            c, s = ORDER[l][v % NC], (v // NC) % 2
            sp.wait_ge(asem(l, "max_row_copied"), T.units(v + 1))
            for a in range(PARTS):
                dst = QS[s][SHIFT_ROW + a:SHIFT_ROW + a + 1, c * C:(c + 1) * C].rearrange("p (t n) -> p t n", t=TC)
                sp.dma_start(dst, max_row[a * TC:(a + 1) * TC, v % 2, :]).then_inc(asem(l, "max_shift"), 16)

        def sp_attention(sp, l):
            sp.wait_ge(sem(f"parts_stored{l}"), 2 * NC * 16)
            sp_operands(sp, l, 0, 0)
            sp_max_rows(sp, l, Turn(l, 0), 0)

            def body(T, first, last):
                for j, s, c, step0, ahead in units(l, first, last):
                    if j % NC == 0 and not (last and s == 1):
                        if not (first and s == 0):
                            sp.wait_ge(asem(l, "weighed"), T.steps(s * STEPS[l]))
                        sp_operands(sp, l, T.heads(s + 1), (s + 1) % 2)
                    if not (last and j == 2 * NC - 1):
                        sp_max_rows(sp, l, T, j + 1)

            pairs(sp, l, body)

        def dve_front(dve, l):
            dve.sem_inc(sem(f"parts_ready{l}"), 1)
            with loop(dve, [link_chain, var_chain, std_chain], [3, 1, 1]) as c:
                dve_norm(dve, lambda t: tile_of(X, c, t))
                for t in range(TC):
                    ins = dve_scale(tile_of(XN, c, t), tile_of(X, c, t), t)
                ins.then_inc(sem(f"xn_ready{l}"), 1)
            with loop(dve, [link_chain], [6]) as c:
                for i, parts in ((0, QP), (1, KP)):
                    dve.wait_ge(sem(f"qk_biased{l}"), c * 2 + (i + 1))
                    p = [parts[:, a, cols(c)] for a in range(PARTS)]
                    dve_link(dve, nc.vector.tensor_copy(p[0], QF[i]))
                    dve_link(dve, nc.vector.tensor_tensor(QR[i], QF[i], p[0], ALU.subtract))
                    dve_link(dve, nc.vector.tensor_copy(p[1], QR[i]))
                    nc.vector.tensor_tensor(p[2], QR[i], p[1], ALU.subtract).then_inc(sem(f"parts_ready{l}"), 1)
                dve.wait_ge(sem(f"v_ready{l}"), c + 1)
                dst = V[:, bass.ds(c * TC, TC), :, 0:HD]
                src = bank(3).rearrange("p (t h d) -> p t h d", t=TC, h=H)
                if l == 0:
                    ins = nc.vector.tensor_copy(dst, src)
                else:
                    b = bias_bc[:, 1, :].rearrange("p (h d) -> p h d", h=H).unsqueeze(1).broadcast_to((P, TC, H, HD))
                    ins = nc.vector.tensor_tensor(dst, src, b, ALU.add)
                ins.then_inc(sem(f"v_taken{l}"), 1)

        def pe_transposes(src, b):
            for t in range(TC):
                ins = nc.tensor.transpose(PS[:, b * C + t * P:b * C + (t + 1) * P], src(t), ident[:, :])
            return ins

        def pe_front(pe, l):
            for c in range(NC):
                pe.wait_ge(sem(f"xn_ready{l}"), c + 1)
                pe.wait_ge(sem(f"xt_ready{l}"), c)
                pe_transposes(lambda t: tile_of(XN, c, t), 0).then_inc(sem(f"x_transposed{l}"), 1)
                pe.wait_ge(sem(f"xt_ready{l}"), c + 1)
                for i, w in ((0, W_Q[l]), (1, W_K[l])):
                    pe.wait_ge(sem(f"qk_biased{l}"), c * 2)
                    nc.tensor.matmul(bank(1 + i), WT[:, w, :], XT[:, cols(c)], start=True, stop=True)\
                        .then_inc(sem(f"qk_ready{l}"), 1)
                pe.wait_ge(sem(f"v_taken{l}"), c)
                for t in range(TC):
                    ins = nc.tensor.matmul(PS[:, 3 * C + t * P:3 * C + (t + 1) * P], XT[:, cols(c, t, P)],
                                           WT[:, W_V[l], :], start=True, stop=True)
                ins.then_inc(sem(f"v_ready{l}"), 1)

        def act_front(act, l):
            with loop(act, act_norms, [1, 1]) as c:
                act_std(act)
            with act.Fori(0, NC) as c:
                act.wait_ge(sem(f"x_transposed{l}"), c + 1)
                nc.scalar.copy(XT[:, cols(c)], bank(0)).then_inc(sem(f"xt_ready{l}"), 1)
                for i in range(2):
                    act.wait_ge(sem(f"qk_ready{l}"), c * 2 + (i + 1))
                    act.wait_ge(sem(f"parts_ready{l}"), c * 2 + 1)
                    if l == 0:
                        ins = nc.scalar.copy(QF[i], bank(1 + i))
                    else:
                        ins = nc.scalar.activation(QF[i], bank(1 + i), ACT.Identity, bias=bias_qk[:, i:i + 1])
                    ins.then_inc(sem(f"qk_biased{l}"), 1)

        def sp_front(sp, l):
            with sp.Fori(0, NC) as c:
                for i, (parts, dst) in enumerate(((QP, QD[l]), (KP, KD[l]))):
                    sp.wait_ge(sem(f"parts_ready{l}"), c * 2 + (i + 2))
                    sp.dma_start(dst[:, :, cols(c)].rearrange("a p n -> p a n"), parts[:, :, cols(c)])\
                        .then_inc(sem(f"parts_stored{l}"), 16)

        def pe_project(pe, l):
            pe.wait_ge(asem(l, "o_used"), H * NC)
            for c in range(NC):
                pe.wait_ge(sem(f"ot_ready{l}"), c)
                pe_transposes(lambda t: tile_of(ON, c, t), 0).then_inc(sem(f"ot_transposed{l}"), 1)
                pe.wait_ge(sem(f"ot_ready{l}"), c + 1)
                pe.wait_ge(sem(f"y_taken{l}"), c)
                for t in range(TC):
                    ins = nc.tensor.matmul(PS[:, C + t * P:C + (t + 1) * P], XT[:, cols(c, t, P)],
                                           WT[:, W_O[l], :], start=True, stop=True)
                ins.then_inc(sem(f"y_ready{l}"), 1)

        def act_project(act, l):
            with loop(act, act_norms, [1, 1]) as c:
                act.wait_ge(sem(f"ot_transposed{l}"), c + 1)
                nc.scalar.copy(XT[:, cols(c)], bank(0)).then_inc(sem(f"ot_ready{l}"), 1)
                act_std(act)

        def dve_project(dve, l):
            bias = bias_bc[:, 0 if l == 0 else 2, :].unsqueeze(1).broadcast_to((P, TC, P))
            with loop(dve, [link_chain, var_chain, std_chain], [5, 1, 1]) as c:
                dve.wait_ge(sem(f"y_ready{l}"), c + 1)
                ins = nc.vector.tensor_tensor(chunk_of(XN, c), bank(1).rearrange("p (t n) -> p t n", t=TC), bias,
                                              ALU.add)
                ins.then_inc(sem(f"y_taken{l}"), 1)
                dve.wait_ge(sem(f"y_taken{l}"), c + 1)
                dve_norm(dve, lambda t: tile_of(XN, c, t))
                dve_residual(dve, c)

        def dve_residual(dve, c):
            for t in range(TC):
                ins = dve_scale(tile_of(XN, c, t), tile_of(XN, c, t), t)
            dve_link(dve, ins)
            dve_link(dve, nc.vector.tensor_tensor(chunk_of(X, c), chunk_of(X, c), chunk_of(XN, c), ALU.add))

        def dve_pick(dve):
            with loop(dve, [link_chain, var_chain, std_chain], [3, 1, 1]) as c:
                dve_norm(dve, lambda t: tile_of(X, c, t))
                for t in range(TC):
                    ins = dve_scale(tile_of(XN, c, t), tile_of(X, c, t), t)
                ins.then_inc(sem("pick_xn"), 1)
            with loop(dve, [link_chain, var_chain, std_chain], [4 + 2 * TC + 5, 1, 1]) as c:
                dve.wait_ge(sem("pick_scores"), c + 1)
                s = bank(1)[:, 0:TC * NE].rearrange("p (t e) -> p t e", t=TC)

                def bc(v):
                    return v.unsqueeze(2).broadcast_to((P, TC, NE))

                dve_link(dve, nc.vector.tensor_reduce(sc_max[:, :], s, AX.X, ALU.max))
                dve_link(dve, nc.vector.tensor_tensor(sc_hit[:, :, :], s, bc(sc_max[:, :]), ALU.is_equal))
                nc.vector.tensor_tensor(sc_hit[:, :, :], sc_hit[:, :, :], tie[:, :, :], ALU.mult)\
                    .then_inc(sem("pick_hit"), 1)
                dve.wait_ge(sem("pick_hit"), c + 1)
                dve_link(dve, nc.vector.tensor_reduce(sc_max[:, :], sc_hit[:, :, :], AX.X, ALU.max))
                dve_link(dve, nc.vector.tensor_tensor(onehot[:, :, :], sc_hit[:, :, :], bc(sc_max[:, :]), ALU.is_equal))
                for t in range(TC):
                    dve.wait_ge(sem("pick_experts"), c * TC + (t + 1))
                    b = bank(2 + 2 * (t % 2), 2).rearrange("p (e f) -> p e f", e=NE)
                    oh = onehot[:, t, :].unsqueeze(2).broadcast_to((P, NE, P))
                    nc.vector.tensor_tensor(picked, b, oh, ALU.mult).then_inc(sem("pick_taken"), 1)
                    dve.wait_ge(sem("pick_taken"), c * TC + (t + 1))
                    dve_link(dve, nc.vector.tensor_reduce(QF[0][:, 0:P], picked.rearrange("p e f -> p f e"), AX.X,
                                                          ALU.add))
                    x = tile_of(XN, c, t)
                    dve_link(dve, nc.vector.tensor_tensor(x, x, QF[0][:, 0:P], ALU.add))
                dve_norm(dve, lambda t: tile_of(XN, c, t))
                dve_residual(dve, c)

        def pe_pick(pe):
            for c in range(NC):
                pe.wait_ge(sem("pick_xn"), c + 1)
                pe.wait_ge(sem("pick_xt"), c)
                pe_transposes(lambda t: tile_of(XN, c, t), 0).then_inc(sem("pick_transposed"), 1)
                pe.wait_ge(sem("pick_xt"), c + 1)
                pe.wait_ge(sem("pick_hit"), c)
                for t in range(TC):
                    ins = nc.tensor.matmul(PS[:, C + t * NE:C + (t + 1) * NE], XT[:, cols(c, t, P)], gateT[:, :],
                                           start=True, stop=True)
                ins.then_inc(sem("pick_scores"), 1)
                for t in range(TC):
                    if t >= 2:
                        pe.wait_ge(sem("pick_taken"), c * TC + (t - 1))
                    else:
                        pe.wait_ge(sem("pick_taken"), c * TC)
                    for i in range(2):
                        w = WT[:, W_E + 4 * i:W_E + 4 * (i + 1), :].rearrange("p e f -> p (e f)")
                        ins = nc.tensor.matmul(bank(2 + 2 * (t % 2) + i), XT[:, cols(c, t, P)], w, start=True, stop=True)
                    ins.then_inc(sem("pick_experts"), 1)

        def act_pick(act):
            with loop(act, act_norms, [1, 1]) as c:
                act_std(act)
            with loop(act, act_norms, [1, 1]) as c:
                act.wait_ge(sem("pick_transposed"), c + 1)
                nc.scalar.copy(XT[:, cols(c)], bank(0)).then_inc(sem("pick_xt"), 1)
                act_std(act)

        def dve_mix(dve):
            for name in ("mix_xc", "mix_h", "mix_got"):
                dve.sem_inc(sem(name), 1)
            with loop(dve, [link_chain, var_chain, std_chain], [3, 1, 1]) as c:
                dve_norm(dve, lambda t: tile_of(X, c, t))
                for t in range(TC):
                    ins = dve_scale(tile_of(XN, c, t), tile_of(X, c, t), t)
                ins.then_inc(sem("mix_xn"), 1)
            dve.wait_ge(sem("mix_logits"), NC)

            def bc(v):
                return v.unsqueeze(3).broadcast_to((P, NT, 2, NE))

            lg = bank(1)[:, 0:NT * 2 * NE].rearrange("p (t k e) -> p t k e", t=NT, k=2)
            dve_link(dve, nc.vector.tensor_reduce(lred[:, :, :], lg, AX.X, ALU.max))
            nc.vector.tensor_tensor(logit[:, :, :, :], lg, bc(lred[:, :, :]), ALU.subtract).then_inc(sem("mix_shifted"), 1)
            dve.wait_ge(sem("mix_exp"), 2)
            dve_link(dve, nc.vector.tensor_reduce(lred[:, :, :], expo[:, :, :, :], AX.X, ALU.add))
            dve_link(dve, nc.vector.reciprocal(linv[:, :, :], lred[:, :, :]))
            dve_link(dve, nc.vector.tensor_tensor(logit[:, :, :, :], expo[:, :, :, :], bc(linv[:, :, :]), ALU.mult))
            dve_link(dve, nc.vector.tensor_tensor(cw[:, :, :], logit[:, :, 0, :], logit[:, :, 1, :], ALU.mult))
            dve_link(dve, nc.vector.tensor_reduce(lred[:, :, 0], cw[:, :, :], AX.X, ALU.add))
            dve_link(dve, nc.vector.tensor_scalar(linv[:, :, 0], lred[:, :, 0], 1e-9, None, ALU.add))
            dve_link(dve, nc.vector.reciprocal(lred[:, :, 1], linv[:, :, 0]))
            nc.vector.tensor_tensor(cw[:, :, :], cw[:, :, :], lred[:, :, 1].unsqueeze(2).broadcast_to((P, NT, NE)),
                                    ALU.mult).then_inc(sem("mix_cw"), 1)
            with dve.Fori(0, NC // 2) as cc:
                link_chain.enter(cc, 8)
                var_chain.enter(cc, 2)
                std_chain.enter(cc, 2)
                for k in range(2):
                    dve_mix_chunk(dve, cc, k)
            for ch in (link_chain, var_chain, std_chain):
                ch.leave(NC // 2)

        def dve_mix_chunk(dve, cc, k):
            c = cc * 2 + k

            def weighted(e):
                if e == 0:
                    dve.wait_ge(sem(f"cw_loaded{k}"), cc * 16 + 16)
                if e >= 2:
                    dve.wait_ge(sem("mix_u"), c * 32 + (4 * e - 3))
                else:
                    dve.wait_ge(sem("mix_u"), c * 32 + 1)
                nc.vector.tensor_tensor(XC[e % 2], XT[:, cols(c)], CWB[k][:, e, :], ALU.mult).then_inc(sem("mix_xc"), 1)

            weighted(0)
            for i in range(32):
                if i % FB == 0 and i // FB + 1 < NE:
                    weighted(i // FB + 1)
                dve.wait_ge(sem("mix_silu"), c * 32 + (i + 2))
                dve.wait_ge(sem("mix_u"), c * 32 + (i + 2))
                if i >= 4:
                    dve.wait_ge(sem("mix_down"), c * 32 + (i - 3))
                nc.vector.tensor_tensor(HB[i % 4], SG[i % 4], bank(4 + i % 2), ALU.mult).then_inc(sem("mix_h"), 1)
            dve.wait_ge(sem("mix_back"), c + 1)
            nc.vector.tensor_copy(chunk_of(XN, c), bank(0).rearrange("p (t n) -> p t n", t=TC)).then_inc(sem("mix_got"), 1)
            dve.wait_ge(sem("mix_got"), c + 2)
            dve_norm(dve, lambda t: tile_of(XN, c, t))
            for t in range(TC):
                ins = dve_scale(tile_of(XN, c, t), tile_of(XN, c, t), t)
            dve_link(dve, ins)
            nc.vector.tensor_tensor(chunk_of(X, c), chunk_of(X, c), chunk_of(XN, c), ALU.add).then_inc(sem("x_final"), 1)

        def act_mix(act):
            for name in ("mix_silu", "mix_out"):
                act.sem_inc(sem(name), 1)
            with loop(act, act_norms, [1, 1]) as c:
                act_std(act)
            with act.Fori(0, NC) as c:
                act.wait_ge(sem("mix_transposed"), c + 1)
                nc.scalar.copy(XT[:, cols(c)], bank(0)).then_inc(sem("mix_xt"), 1)
            act.wait_ge(sem("mix_shifted"), 1)
            nc.scalar.activation(expo[:, :, 0, :], logit[:, :, 0, :], ACT.Exp).then_inc(sem("mix_exp"), 1)
            nc.scalar.activation(expo[:, :, 1, :], logit[:, :, 1, :], ACT.Exp, scale=1.0 / GATE_TEMP)\
                .then_inc(sem("mix_exp"), 1)
            act.wait_ge(sem("cw_transposed"), 1)
            nc.scalar.copy(cwT[:, :], bank(0)[:, 0:P]).then_inc(sem("cw_rows"), 1)
            with loop(act, act_norms, [1, 1]) as c:
                for i in range(32):
                    act.wait_ge(sem("mix_g"), c * 32 + (i + 1))
                    if i >= 4:
                        act.wait_ge(sem("mix_h"), c * 32 + (i - 2))
                    nc.scalar.activation(SG[i % 4], bank(2 + i % 2), ACT.Silu).then_inc(sem("mix_silu"), 1)
                act.wait_ge(sem("mix_down"), c * 32 + 32)
                nc.scalar.copy(o_sb[:, 0, :], bank(6)).then_inc(sem("mix_out"), 1)
                act_std(act)

        def pe_mix(pe):
            pe.sem_inc(sem("mix_u"), 1)
            for c in range(NC):
                pe.wait_ge(sem("mix_xn"), c + 1)
                pe.wait_ge(sem("mix_xt"), c)
                pe_transposes(lambda t: tile_of(XN, c, t), 0).then_inc(sem("mix_transposed"), 1)
                pe.wait_ge(sem("mix_xt"), c + 1)
                for t in range(TC):
                    ins = nc.tensor.matmul(PS[:, bass.ds(c * (TC * 2 * NE) + (C + t * 2 * NE), 2 * NE)],
                                           XT[:, cols(c, t, P)], rgw[:, :, :].rearrange("p k e -> p (k e)"),
                                           start=True, stop=True)
                ins.then_inc(sem("mix_logits"), 1)
            pe.wait_ge(sem("mix_cw"), 1)
            nc.tensor.transpose(bank(0)[:, 0:P], cw[:, :, :].rearrange("p t e -> p (t e)"), ident[:, :])\
                .then_inc(sem("cw_transposed"), 1)
            with pe.Fori(0, NC) as c:
                def down(i):
                    pe.wait_ge(sem("mix_h"), c * 32 + (i + 2))
                    if i == 0:
                        pe.wait_ge(sem("mix_out"), c + 1)
                        pe.wait_ge(sem("wd_loaded"), 16)
                    nc.tensor.matmul(bank(6), Wd[:, i, :], HB[i % 4], start=i == 0, stop=i == 31)\
                        .then_inc(sem("mix_down"), 1)

                for i in range(32):
                    e, f = divmod(i, FB)
                    pe.wait_ge(sem("mix_silu"), c * 32 + max(i, 1))
                    nc.tensor.matmul(bank(2 + i % 2), Wg[:, e, f * P:(f + 1) * P], XT[:, cols(c)], start=True, stop=True)\
                        .then_inc(sem("mix_g"), 1)
                    pe.wait_ge(sem("mix_h"), c * 32 + max(i, 1))
                    if f == 0:
                        pe.wait_ge(sem("mix_xc"), c * NE + (e + 2))
                    nc.tensor.matmul(bank(4 + i % 2), Wu[:, e, f * P:(f + 1) * P], XC[e % 2], start=True, stop=True)\
                        .then_inc(sem("mix_u"), 1)
                    if i >= 1:
                        down(i - 1)
                down(31)
                pe.wait_ge(sem("mix_out"), c + 2)
                pe.wait_ge(sem("cw_rows"), 1)
                pe.wait_ge(sem("mix_got"), c + 1)
                pe_transposes(lambda t: o_sb[:, 0, t * P:(t + 1) * P], 0).then_inc(sem("mix_back"), 1)

        def sp_mix(sp):
            sp.wait_ge(sem("x_transposed1"), NC)
            sp.wait_ge(asem(1, "o_used"), H * NC)
            sp.dma_start(Wd[:, :, :], w_down.rearrange("e (f p) h -> p (e f) h", p=P)).then_inc(sem("wd_loaded"), 16)
            sp.wait_ge(sem("cw_rows"), 1)
            for t in range(NT):
                sp.dma_start(CD[:, t * P:(t + 1) * P], cwT[t * NE:(t + 1) * NE, :]).then_inc(sem("cw_stored"), 16)
            sp.wait_ge(sem("cw_stored"), NT * 16)
            out_v = out[0].rearrange("(t p) d -> p t d", p=P)

            def load(c):
                if c >= 2:
                    sp.wait_ge(sem("mix_xc"), 1 + (c - 1) * NE)
                src = bass.AP(CD.tensor, c * C, [[0, P], [N, NE], [1, C]])
                sp.dma_start(CWB[c % 2], src).then_inc(sem(f"cw_loaded{c % 2}"), 16)

            load(0)
            load(1)
            for c in range(NC):
                if c + 2 < NC:
                    load(c + 2)
                sp.wait_ge(sem("x_final"), c + 1)
                sp.dma_start(out_v[:, c * TC:(c + 1) * TC, :], chunk_of(X, c)).then_inc(sem("stored"), 16)
            sp.wait_ge(sem("stored"), NC * 16)

        CONSTS, PADS = 4 + NE, 5
        block = ctx.enter_context(nc.Block())

        @block.sync
        def _(sp):
            sp.dma_start(X[:, :, :], x_in[0].rearrange("(t p) d -> p t d", p=P)).then_inc(sem("x_loaded"), 16)
            sp.dma_start(raw[:, 0:3, :], w_qkv.rearrange("(b p) c -> p b c", p=P)).then_inc(sem("w_loaded"), 16)
            for i, w in ((3, w_proj), (4, Wq), (5, Wk), (6, Wv), (7, Wo)):
                sp.dma_start(raw[:, i, :], w).then_inc(sem("w_loaded"), 16)
            sp.dma_start(raw[:, W_E:W_E + NE, :], expert_w.rearrange("e f h -> f e h")).then_inc(sem("w_loaded"), 16)
            sp.dma_start(raw_gate, gate_w).then_inc(sem("w_loaded"), 16)
            for i, b in enumerate((b_proj, bv, bo)):
                sp.dma_start(bias_bc[:, i, :], b.partition_broadcast(P)).then_inc(sem("b_loaded"), 16)
            for i, b in enumerate((bq, bk)):
                sp.dma_start(bias_qk[:, i:i + 1], b.rearrange("(p a) -> p a", a=1)).then_inc(sem("b_loaded"), 16)
            for i, w in enumerate((w_router, w_gating)):
                sp.dma_start(rgw[:, i, :], w).then_inc(sem("b_loaded"), 16)
            sp.dma_start(Wg[:, :, :], w_gate.rearrange("e h f -> h e f")).then_inc(sem("wgu_loaded"), 16)
            sp.dma_start(Wu[:, :, :], w_up.rearrange("e h f -> h e f")).then_inc(sem("wgu_loaded"), 16)
            sp_front(sp, 0)
            sp_attention(sp, 0)
            sp_front(sp, 1)
            sp_attention(sp, 1)
            sp_mix(sp)

        @block.gpsimd
        def _(pool):
            nc.gpsimd.memset(ident[:, :], 0.0).then_inc(sem("zeroed"), 1)
            nc.gpsimd.memset(identb[:, :], 0.0).then_inc(sem("zeroed"), 1)
            nc.gpsimd.memset(mask_nat[:, :], 0.0).then_inc(sem("zeroed"), 1)
            nc.gpsimd.memset(mask_t[:, :], 0.0).then_inc(sem("zeroed"), 1)
            pool.wait_ge(sem("zeroed"), 4)
            for m in (ident, identb):
                nc.gpsimd.affine_select(out=m[:, :], in_=m[:, :], compare_op=ALU.not_equal, fill=1.0, base=0,
                                        pattern=[[-1, P]], channel_multiplier=1).then_inc(sem("consts"), 1)
            nc.gpsimd.affine_select(out=mask_nat[:, :], in_=mask_nat[:, :], compare_op=ALU.is_ge, fill=MASKED, base=0,
                                    pattern=[[-1, P]], channel_multiplier=1).then_inc(sem("consts"), 1)
            nc.gpsimd.affine_select(out=mask_t[:, :], in_=mask_t[:, :], compare_op=ALU.is_ge, fill=MASKED, base=0,
                                    pattern=[[1, P]], channel_multiplier=-1).then_inc(sem("consts"), 1)
            for e in range(NE):
                nc.gpsimd.memset(tie[:, :, e], float(NE - e)).then_inc(sem("consts"), 1)
            for s in range(2):
                nc.gpsimd.memset(VH[s], 0.0).then_inc(sem("v_zeroed"), 1)
                pool.wait_ge(sem("v_zeroed"), s + 1)
                nc.gpsimd.memset(VH[s][:, :, HD], 1.0).then_inc(sem("pads"), 1)
                nc.gpsimd.memset(QS[s], 0.0).then_inc(sem("pads"), 1)
                nc.gpsimd.memset(KS[s], 0.0).then_inc(sem("ks_zeroed"), 1)
                pool.wait_ge(sem("ks_zeroed"), s + 1)
                nc.gpsimd.memset(KS[s][SHIFT_ROW:P, :], 1.0).then_inc(sem("ks_ones"), 1)
                pool.wait_ge(sem("ks_ones"), s + 1)
            nc.gpsimd.memset(probs_diag[:, :, :], 0.0).then_inc(sem("pads"), 1)
            pool.wait_ge(sem("pads"), PADS)
            pool_attention(pool, 0)
            pool_attention(pool, 1)

        @block.scalar
        def _(act):
            for b in range(4):
                act.wait_ge(sem("w_transposed"), b + 1)
                nc.scalar.copy(WT[:, 4 * b:4 * b + 4, :].rearrange("p b c -> p (b c)"), bank(b + 1))\
                    .then_inc(sem("w_ready"), 1)
            act.wait_ge(sem("w_transposed"), 5)
            nc.scalar.copy(gateT[:, :], bank(5)[:, 0:NE]).then_inc(sem("w_ready"), 1)
            act.wait_ge(sem("b_loaded"), 7 * 16)
            act_front(act, 0)
            act.wait_ge(sem("pads"), PADS)
            act_attention(act, 0)
            act_project(act, 0)
            act_pick(act)
            act_front(act, 1)
            act_attention(act, 1)
            act_project(act, 1)
            act_mix(act)

        @block.vector
        def _(dve):
            nc.vector.memset(held[:, :], 0.0).then_inc(sem("held_ready"), 1)
            dve.wait_ge(sem("held_ready"), 1)
            dve.wait_ge(sem("x_loaded"), 16)
            dve.wait_ge(sem("b_loaded"), 7 * 16)
            dve.wait_ge(sem("consts"), CONSTS)
            dve.wait_ge(sem("pads"), PADS)
            dve_front(dve, 0)
            dve_attention(dve, 0)
            dve_project(dve, 0)
            dve_pick(dve)
            dve_front(dve, 1)
            dve_attention(dve, 1)
            dve_project(dve, 1)
            dve_mix(dve)

        @block.tensor
        def _(pe):
            pe.wait_ge(sem("consts"), CONSTS)
            pe.wait_ge(sem("w_loaded"), 8 * 16)
            for b in range(4):
                for i in range(4):
                    ins = nc.tensor.transpose(PS[:, (b + 1) * C + i * P:(b + 1) * C + (i + 1) * P], raw[:, 4 * b + i, :],
                                              ident[:, :])
                ins.then_inc(sem("w_transposed"), 1)
            nc.tensor.transpose(bank(5)[:, 0:NE], raw_gate, ident[0:NE, 0:NE]).then_inc(sem("w_transposed"), 1)
            pe.wait_ge(sem("w_ready"), 5)
            pe.wait_ge(sem("b_loaded"), 7 * 16)
            pe.wait_ge(sem("pads"), PADS)
            pe.wait_ge(sem("wgu_loaded"), 32)
            pe_front(pe, 0)
            pe_attention(pe, 0)
            pe_project(pe, 0)
            pe_pick(pe)
            pe_front(pe, 1)
            pe_attention(pe, 1)
            pe_project(pe, 1)
            pe_mix(pe)


INS = ['L0_attn_x', 'L0_attn_w_qkv', 'L0_attn_w_proj', 'L0_attn_b_proj', 'L0_ffn_gate_w', 'L0_ffn_expert_w',
       'L1_attn_Wq', 'L1_attn_bq', 'L1_attn_Wk', 'L1_attn_bk', 'L1_attn_Wv', 'L1_attn_bv', 'L1_attn_Wo', 'L1_attn_bo',
       'L1_ffn_w_router', 'L1_ffn_w_gating', 'L1_ffn_w_gate', 'L1_ffn_w_up', 'L1_ffn_w_down']


def kernel(**inputs):
    import numpy as np
    import concourse.bacc as bacc
    from concourse.bass_utils import run_bass_kernel_spmd

    nc = bacc.Bacc("TRN2", target_bir_lowering=False, num_devices=1)
    arrays, args = {}, []
    for name in INS:
        a = np.ascontiguousarray(inputs[name])
        arrays[f"in_{name}"] = a
        args.append(nc.dram_tensor(f"in_{name}", a.shape, mybir.dt.from_np(a.dtype), kind="ExternalInput").ap())
    out = nc.dram_tensor("out", (1, N, P), FP32, kind="ExternalOutput").ap()
    sandwich(nc, *args, out)
    r = run_bass_kernel_spmd(nc, [arrays], core_ids=[0])
    return r.results[0]["out"]
```

```python
import concourse.bass as bass
from concourse import mybir
from contextlib import ExitStack

FP32 = mybir.dt.float32
BF16 = mybir.dt.bfloat16
ALU = mybir.AluOpType
ACT = mybir.ActivationFunctionType
AX = mybir.AxisListType

P = 128
N = 2048
NT = N // P
C = 512
NC = N // C
TC = C // P
H = 16
HD = P // H
SCALE = HD ** -0.5
NE = 8
F = 512
FB = F // P
LN_EPS = 1e-5
MASKED = -9e15
GATE_TEMP = 0.1

PARTS = 3
ROWS = PARTS * PARTS * HD
NAT_ROWS = 96
SHIFT_ROW = 96
T_ROWS = SHIFT_ROW + PARTS


class Chain:

    def __init__(self, sem):
        self.sem, self.n, self.turn, self.per, self.start = sem, 0, None, 0, 0

    def enter(self, turn, per):
        self.turn, self.per, self.start = turn, per, self.n

    def leave(self, turns):
        assert self.n - self.start == self.per, (self.n - self.start, self.per)
        self.n, self.turn = self.start + self.per * turns, None

    def value(self):
        return self.n if self.turn is None else self.turn * self.per + self.n


def sandwich(nc, x_in, w_qkv, w_proj, b_proj, gate_w, expert_w, Wq, bq, Wk, bk, Wv, bv, Wo, bo,
             w_router, w_gating, w_gate, w_up, w_down, out):
    ctx = ExitStack()
    with ctx:
        def sb(name, shape, dt=FP32):
            return ctx.enter_context(nc.sbuf_tensor(name, shape, dt))

        sems = {}

        def sem(name):
            if name not in sems:
                sems[name] = ctx.enter_context(nc.semaphore(name))
            return sems[name]

        X = sb("X", [P, NT, P])
        XN = sb("XN", [P, NT, P])
        XT = sb("XT", [P, N])
        ON = sb("ON", [P, NT, P])
        ident = sb("ident", [P, P])
        identb = sb("identb", [P, P], BF16)
        mask_nat = sb("mask_nat", [P, P], BF16)
        mask_t = sb("mask_t", [P, P], BF16)
        WT = sb("WT", [P, 16, P])
        gateT = sb("gateT", [P, NE])
        rgw = sb("rgw", [P, 2, NE])
        bias_bc = sb("bias_bc", [P, 3, P])
        bias_qk = sb("bias_qk", [P, 2])
        Wg = sb("Wg", [P, NE, F])
        Wu = sb("Wu", [P, NE, F])
        probs = sb("probs", [P, 4, C])
        probs_diag = sb("probs_diag", [P, TC, C])
        o_sb = sb("o_sb", [P, 2, C])
        max_row = sb("max_row", [P, 4, P], BF16)
        stats = sb("stats", [P, TC, 6])
        held = sb("held", [P, 2])
        mv = sb("mv", [P, TC, 2])
        var_eps = sb("var_eps", [P, TC])
        std = sb("std", [P, TC])
        rstd = sb("rstd", [P, TC])
        mx = sb("mx", [P, 4, TC, 2])
        zeros = sb("zeros", [P, TC])
        neg_max = sb("neg_max", [P, 4, TC])
        rest1 = sb("rest1", [P, TC])
        max_parts = sb("max_parts", [P, 4, PARTS, TC], BF16)
        osum = sb("osum", [P, TC, HD + 1])
        oinv = sb("oinv", [P, TC])
        logit = sb("logit", [P, NT, 2, NE])
        expo = sb("expo", [P, NT, 2, NE])
        lred = sb("lred", [P, NT, 2])
        linv = sb("linv", [P, NT, 2])
        cw = sb("cw", [P, NT, NE])
        cwT = sb("cwT", [P, P])
        tie = sb("tie", [P, TC, NE])
        sc_max = sb("sc_max", [P, TC])
        sc_hit = sb("sc_hit", [P, TC, NE])
        onehot = sb("onehot", [P, TC, NE])

        A = sb("A", [P, 20480])
        V = A[:, 0:2048].rearrange("p (t h d) -> p t h d", t=NT, h=H)
        VH = [A[:, 2048 + 512 * s:2560 + 512 * s].rearrange("p (t d) -> p t d", t=NT)
              for s in range(2)]
        QS = [A[:, 8192 + 1024 * s:8192 + 1024 * (s + 1)].bitcast(BF16) for s in range(2)]
        KS = [A[:, 10240 + 1024 * s:10240 + 1024 * (s + 1)].bitcast(BF16) for s in range(2)]
        QP = A[:, 12288:15360].bitcast(BF16).rearrange("p (a n) -> p a n", a=PARTS)
        KP = A[:, 15360:18432].bitcast(BF16).rearrange("p (a n) -> p a n", a=PARTS)
        QF = [A[:, 18432 + C * i:18432 + C * (i + 1)] for i in range(2)]
        QR = [A[:, 19456 + C * i:19456 + C * (i + 1)] for i in range(2)]
        raw = A[:, 12288:14336].rearrange("p (b c) -> p b c", b=16)
        raw_gate = A[0:NE, 14336:14336 + P]
        picked = A[:, 12288:12288 + NE * P].rearrange("p (e f) -> p e f", e=NE)
        CWB = [A[:, 4096 * i:4096 * (i + 1)].rearrange("p (e n) -> p e n", e=NE) for i in range(2)]
        HB = [A[:, 8192 + C * i:8192 + C * (i + 1)] for i in range(4)]
        SG = [A[:, 10240 + C * i:10240 + C * (i + 1)] for i in range(4)]
        XC = [A[:, 12288 + C * i:12288 + C * (i + 1)] for i in range(2)]
        Wd = A[:, 16384:20480].rearrange("p (k h) -> p k h", h=P)

        W_Q, W_K, W_V, W_O = (0, 4), (1, 5), (2, 6), (3, 7)
        W_E = 8

        PS = ctx.enter_context(nc.psum_tensor("PS", [P, 8 * C], FP32))

        def bank(i, n=1):
            return PS[:, i * C:(i + n) * C]

        QD = [nc.dram_tensor(f"q_parts{l}", (PARTS, P, N), BF16, kind="Internal").ap() for l in range(2)]
        KD = [nc.dram_tensor(f"k_parts{l}", (PARTS, P, N), BF16, kind="Internal").ap() for l in range(2)]
        CD = nc.dram_tensor("cw_rows", (NE, N), FP32, kind="Internal").ap()

        link_sem = sem("dve_link")
        link_chain = Chain(link_sem)
        var_chain, std_chain = Chain(sem("var_ready")), Chain(sem("std_ready"))
        act_norms = [Chain(sem("var_ready")), Chain(sem("std_ready"))]

        def dve_link(dve, ins):
            link_chain.n += 1
            ins.then_inc(link_chain.sem, 1)
            dve.wait_ge(link_chain.sem, link_chain.value())

        def hold_wait():
            nc.vector.tensor_copy(held[:, 1:2], held[:, 0:1])

        def dve_norm(dve, src, ready=None):
            hold_wait()
            for t in range(TC):
                ins = nc.vector.bn_stats(stats[:, t, :], src(t))
            dve_link(dve, ins)
            hold_wait()
            for t in range(TC):
                ins = nc.vector.bn_aggr(mv[:, t, :], stats[:, t, :])
            dve_link(dve, ins)
            var_chain.n += 1
            nc.vector.tensor_scalar(var_eps[:, :], mv[:, :, 1], LN_EPS, None, ALU.add).then_inc(var_chain.sem, 1)
            std_chain.n += 1
            dve.wait_ge(std_chain.sem, std_chain.value())
            dve_link(dve, nc.vector.reciprocal(rstd[:, :], std[:, :]))

        def dve_scale(dst, src, t):
            return nc.vector.tensor_scalar(dst, src, mv[:, t, 0:1], rstd[:, t:t + 1],
                                           ALU.subtract, ALU.mult)

        def act_std(act):
            v, s = act_norms
            v.n += 1
            s.n += 1
            act.wait_ge(v.sem, v.value())
            nc.scalar.activation(std[:, :], var_eps[:, :], ACT.Sqrt).then_inc(s.sem, 1)

        def tile_of(buf, c, t):
            return buf[:, c * TC + t, :]

        def chunk_of(buf, c):
            return buf[:, bass.ds(c * TC, TC), :]

        def cols(c, t=0, n=C):
            return bass.ds(c * C + t * P, n)

        def loop(eng, chains, per, turns=NC):
            class L:
                def __enter__(s):
                    s.f = eng.Fori(0, turns)
                    i = s.f.__enter__()
                    for ch, p in zip(chains, per):
                        ch.enter(i, p)
                    return i

                def __exit__(s, *a):
                    for ch in chains:
                        if a[0] is None:
                            ch.leave(turns)
                    return s.f.__exit__(*a)
            return L()

        ORDER = [[0, 1, 2, 3], [3, 2, 1, 0]]
        LEAD = 3
        TURN = 2 * NC
        OPERANDS = 2 * PARTS * 16

        def chunk(l, j):
            return ORDER[l][j % NC]

        def key_tiles(l, j):
            return NT if l == 0 else TC * (chunk(l, j) + 1)

        def steps_before(l, j):
            return sum(key_tiles(l, u) for u in range(j))

        def max_items(l, j):
            items, c = [], chunk(l, j)
            for t in range(TC):
                n = N if l == 0 else (TC * c + t + 1) * P
                for s, k0 in enumerate(range(0, n, 2 * C)):
                    pieces = []
                    for k in range(k0, min(k0 + 2 * C, n), C):
                        w = min(C, n - k)
                        pieces.append((k, w, l == 1 and k + w == n))
                    items.append((t, s, pieces))
            return items

        def items_before(l, j):
            return sum(len(max_items(l, u)) for u in range(j))

        def slots(l, j):
            return 2 if l == 0 or chunk(l, j) >= 2 else 1

        def ahead(l, j, last):
            return [] if last and j + LEAD >= TURN else max_items(l, j + LEAD)

        def items_at(l, j, n, i):
            return [r for r in range(n) if r * key_tiles(l, j) // n == i]

        def out_step(l, j):
            return 3 if key_tiles(l, j) == TC else 5

        def row_events(l, j, last):
            ev = [[[(10, 2)]] * NC, [[(9, 1), (13, 2)], [(8, 2)], [(7, 2)], []]][l][j % NC]
            return [(at, j + d) for at, d in ev if not (last and j + d >= TURN)]

        def row_bank(l, v):
            return 6 + (v % 2 if l == 1 and v % NC == 1 else (v + 1) % 2)

        ROWS_AHEAD = [2, 1]

        STEPS = [steps_before(l, NC) for l in range(2)]
        ITEMS = [items_before(l, NC) for l in range(2)]

        class Turn:

            def __init__(self, l, g):
                self.l, self.g = l, g

            def steps(self, n):
                return self.g * (2 * STEPS[self.l]) + n

            def items(self, n):
                return self.g * (2 * ITEMS[self.l]) + n

            def units(self, n):
                return self.g * TURN + n

            def halves(self, n):
                return self.g * (TURN // 2 * 16) + 16 * n

            def heads(self, n):
                return self.g * 2 + n

        def turns(eng, l, body, chain=None, per=0):
            body(Turn(l, 0), True, False)
            with eng.Fori(1, H // 2 - 1) as g:
                if chain:
                    chain.n -= per
                    chain.enter(g, per)
                body(Turn(l, g), False, False)
            if chain:
                chain.leave(H // 2 - 1)
            body(Turn(l, H // 2 - 1), False, True)

        def asem(l, name):
            return sem(f"{name}{l}")

        def slot(j):
            return j // NC % 2

        def pe_max_item(pe, l, T, v, r):
            c = chunk(l, v)
            t, _, pieces = max_items(l, v)[r]
            r += items_before(l, v)
            if not (isinstance(T.g, int) and T.g == 0 and r < 2):
                pe.wait_ge(asem(l, "max_taken"), T.items(r - 1))
            at = (r % 2) * 2
            q = QS[slot(v)][0:NAT_ROWS, c * C + t * P:c * C + (t + 1) * P]
            for n, (k, w, diag) in enumerate(pieces):
                dst = PS[:, (at + n) * C:(at + n) * C + w]
                ins = nc.tensor.matmul(dst, q, KS[slot(v)][0:NAT_ROWS, k:k + w], start=True, stop=not diag)
                if diag:
                    ins = nc.tensor.matmul(dst[:, w - P:w], identb[:, :], mask_nat[:, :], start=False, stop=True)
            ins.then_inc(asem(l, "max_scores"), 1)

        def row_psum(l, v):
            return PS[0:PARTS * TC, row_bank(l, v) * C:row_bank(l, v) * C + P // 2].bitcast(BF16)

        def pe_max_rows(pe, l, T, v):
            pe.wait_ge(asem(l, "max_parts_ready"), T.units(v + 1))
            nc.tensor.transpose(row_psum(l, v), max_parts[:, v % 4, :, :].rearrange("p a t -> p (a t)"),
                                identb[:, :]).then_inc(asem(l, "max_rows"), 1)

        def pe_transpose_out(pe, l, T, j):
            pe.wait_ge(asem(l, "o_copied"), T.units(j + 1))
            b = (6 + j % 2) * C
            for t in range(TC):
                ins = nc.tensor.transpose(PS[:, b + t * P:b + (t + 1) * P], o_sb[:, j % 2, t * P:(t + 1) * P],
                                          ident[:, :])
            ins.then_inc(asem(l, "o_transposed"), 1)

        def pe_attention(pe, l):
            pe.wait_ge(sem(f"v_taken{l}"), NC)
            pe.wait_ge(asem(l, "operands"), OPERANDS)
            T0 = Turn(l, 0)
            for v in range(LEAD):
                for r in range(len(max_items(l, v))):
                    pe_max_item(pe, l, T0, v, r)
                if v >= 1 and v - 1 < ROWS_AHEAD[l]:
                    pe_max_rows(pe, l, T0, v - 1)

            def weigh(j, i):
                nk, c = key_tiles(l, j), chunk(l, j)
                diag = l == 1 and i >= nk - TC
                g = i % TC
                q0 = P * g if diag and c > 0 else 0
                src = probs_diag[:, g, q0:C] if diag else probs[:, (steps_before(l, j % TURN) + i) % 4, :]
                b = (6 + j % 2) * C
                nc.tensor.matmul(PS[32 * g:32 * g + 32, b + q0:b + C], VH[slot(j)][:, i, :], src,
                                 start=i < TC, stop=i >= nk - TC, skip_group_check=True)\
                    .then_inc(asem(l, "weighed"), 1)

            def body(T, first, last):
                behind = [] if first else [(TURN - 1, key_tiles(l, TURN - 1) - 2), (TURN - 1, key_tiles(l, TURN - 1) - 1)]
                for j in range(TURN):
                    nk, c, n0 = key_tiles(l, j), chunk(l, j), steps_before(l, j)
                    items = ahead(l, j, last)
                    rows = row_events(l, j, last)
                    for i in range(nk):
                        n = n0 + i
                        if i == out_step(l, j) and not (first and j == 0):
                            pe_transpose_out(pe, l, T, j - 1)
                        for k, (at, v) in enumerate(rows):
                            if i == at:
                                if k:
                                    pe.wait_ge(asem(l, "max_row_copied"), T.units(v))
                                elif not (first and j == 0):
                                    pe.wait_ge(asem(l, "o_used"), T.units(j))
                                pe_max_rows(pe, l, T, v)
                        if i == 0:
                            pe.wait_ge(asem(l, f"max_shift{j % 2}_"), T.halves(j // 2 + 1))
                        if not (first and n < 2):
                            pe.wait_ge(asem(l, "exp_done"), T.steps(n - 1))
                        diag = l == 1 and i >= nk - TC
                        q0 = P * (i % TC) if diag else 0
                        dst = PS[:, (4 + n % 2) * C + q0:(5 + n % 2) * C]
                        ins = nc.tensor.matmul(dst, KS[slot(j)][0:T_ROWS, i * P:(i + 1) * P],
                                               QS[slot(j)][0:T_ROWS, c * C + q0:(c + 1) * C], start=True, stop=not diag)
                        if diag:
                            ins = nc.tensor.matmul(dst[:, 0:P], identb[:, :], mask_t[:, :], start=False, stop=True)
                        ins.then_inc(asem(l, "scores_t"), 1)
                        for r in items_at(l, j, len(items), i) if items else []:
                            if r == 0 and j % NC == NC - LEAD:
                                pe.wait_ge(asem(l, "operands"), T.heads(slot(j) + 2) * OPERANDS)
                            pe_max_item(pe, l, T, j + LEAD, r)
                        if i == 2:
                            if j % NC == 0:
                                pe.wait_ge(asem(l, "values"), T.heads(slot(j) + 1))
                            if not (first and j < 2):
                                pe.wait_ge(asem(l, "o_used"), T.units(j - 1))
                        behind.append((j, i))
                        if n >= 2 or not first:
                            weigh(*behind.pop(0))
                if last:
                    pe.wait_ge(asem(l, "exp_done"), H * STEPS[l])
                    for u in behind:
                        weigh(*u)

            turns(pe, l, body)
            pe_transpose_out(pe, l, Turn(l, H // 2 - 1), TURN - 1)

        def act_out_copy(act, l, T, j):
            act.wait_ge(asem(l, "weighed"), T.steps(steps_before(l, j + 1)))
            nc.scalar.copy(o_sb[:, j % 2, :], bank(6 + j % 2)).then_inc(asem(l, "o_copied"), 1)

        def act_max_rows(act, l, T, v):
            act.wait_ge(asem(l, "max_rows"), T.units(v + 1))
            nc.scalar.copy(max_row[0:PARTS * TC, v % 4, :], row_psum(l, v)).then_inc(asem(l, "max_row_copied"), 1)

        def act_attention(act, l):
            for v in range(ROWS_AHEAD[l]):
                act_max_rows(act, l, Turn(l, 0), v)

            def body(T, first, last):
                for j in range(TURN):
                    nk, n0 = key_tiles(l, j), steps_before(l, j)
                    for i in range(nk):
                        n = n0 + i
                        if i == 3 and not (first and j == 0):
                            act_out_copy(act, l, T, j - 1)
                        for at, v in row_events(l, j, last):
                            if i == at:
                                act_max_rows(act, l, T, v)
                        act.wait_ge(asem(l, "scores_t"), T.steps(n + 1))
                        diag = l == 1 and i >= nk - TC
                        q0 = P * (i % TC) if diag else 0
                        dst = probs_diag[:, i % TC, q0:C] if diag else probs[:, n % 4, :]
                        nc.scalar.activation(dst, PS[:, (4 + n % 2) * C + q0:(5 + n % 2) * C], ACT.Exp,
                                             scale=SCALE).then_inc(asem(l, "exp_done"), 1)

            turns(act, l, body)
            act_out_copy(act, l, Turn(l, H // 2 - 1), TURN - 1)

        def dve_reduce(dve, l, T, v, r):
            t, s, pieces = max_items(l, v)[r]
            r += items_before(l, v)
            w = pieces[-1][0] + pieces[-1][1] - pieces[0][0]
            dve.wait_ge(asem(l, "max_scores"), T.items(r + 1))
            at = (r % 2) * 2 * C
            nc.vector.tensor_reduce(mx[:, v % 4, t, s:s + 1], PS[:, at:at + w], AX.X, ALU.max)\
                .then_inc(asem(l, "max_taken"), 1)

        def dve_neg_max(dve, l, T, v):
            dve.wait_ge(asem(l, "max_taken"), T.items(items_before(l, v + 1)))
            nc.vector.tensor_reduce(neg_max[:, v % 4, :], mx[:, v % 4, :, 0:slots(l, v)], AX.X, ALU.max,
                                    negate=True).then_inc(asem(l, "max_known"), 1)

        def dve_output(dve, l, T, j):
            def total():
                dve.wait_ge(asem(l, "o_transposed"), T.units(j + 1))
                src = bank(6 + j % 2).rearrange("p (t g d) -> p t d g", t=TC, g=4)
                nc.vector.tensor_reduce(osum[:, :, :], src[:, :, 0:HD + 1, :], AX.X, ALU.add)\
                    .then_inc(asem(l, "o_summed"), 1)

            def inverse():
                dve.wait_ge(asem(l, "o_summed"), T.units(j + 1))
                nc.vector.reciprocal(oinv[:, :], osum[:, :, HD]).then_inc(asem(l, "o_inverse"), 1)

            def divide():
                dve.wait_ge(asem(l, "o_inverse"), T.units(j + 1))
                c = chunk(l, j)
                dst = ON[:, c * TC:(c + 1) * TC, bass.ds(T.heads(slot(j) if j >= 0 else -1) * HD, HD)]
                nc.vector.tensor_tensor(dst, osum[:, :, 0:HD], oinv[:, :].unsqueeze(2).broadcast_to((P, TC, HD)),
                                        ALU.mult).then_inc(asem(l, "o_used"), 1)

            return [total, inverse, divide]

        def dve_attention(dve, l):
            T0 = Turn(l, 0)
            for v in range(LEAD):
                for r in range(len(max_items(l, v))):
                    dve_reduce(dve, l, T0, v, r)
                    if r == 0 and v >= 1:
                        dve_neg_max(dve, l, T0, v - 1)

            def body(T, first, last):
                for j in range(TURN):
                    items = ahead(l, j, last)
                    def issued(step):
                        return sum(len(items_at(l, j, len(items), i)) for i in range(step)) if items else 0

                    before = issued(out_step(l, j))
                    limit = min([issued(at) for at, _ in row_events(l, j, last)] + [len(items)])
                    out_ops = [] if first and j == 0 else dve_output(dve, l, T, j - 1)
                    for r in range(len(items)):
                        while out_ops and (r >= limit or r >= before + 3 - len(out_ops)):
                            out_ops.pop(0)()
                        dve_reduce(dve, l, T, j + LEAD, r)
                        if r == 0:
                            dve_neg_max(dve, l, T, j + LEAD - 1)
                    if not items and j + LEAD == TURN:
                        dve_neg_max(dve, l, T, TURN - 1)
                    for op in out_ops:
                        op()

            turns(dve, l, body)
            dve.wait_ge(asem(l, "o_used"), H * NC - 1)
            for op in dve_output(dve, l, Turn(l, H // 2 - 1), TURN - 1):
                op()

        pool_chain = Chain(sem("pool_link"))

        def pool_link(pool, ins):
            pool_chain.n += 1
            ins.then_inc(pool_chain.sem, 1)
            pool.wait_ge(pool_chain.sem, pool_chain.value())

        def pool_max_parts(pool, l, T, v):
            tt = nc.gpsimd.tensor_tensor
            m, x = max_parts[:, v % 4], neg_max[:, v % 4, :]
            pool.wait_ge(asem(l, "max_known"), T.units(v + 1))
            pool_link(pool, tt(m[:, 0, :], x, zeros[:, :], ALU.add))
            pool_link(pool, tt(rest1[:, :], x, m[:, 0, :], ALU.subtract))
            pool_link(pool, tt(m[:, 1, :], rest1[:, :], zeros[:, :], ALU.add))
            tt(m[:, 2, :], rest1[:, :], m[:, 1, :], ALU.subtract).then_inc(asem(l, "max_parts_ready"), 1)

        PART_LINKS = 3

        def pool_attention(pool, l):
            pool.wait_ge(sem(f"v_taken{l}"), NC)

            def values(T, head):
                nc.gpsimd.tensor_copy(VH[head % 2][:, :, 0:HD], V[:, :, T.heads(head), :]).then_inc(asem(l, "values"), 1)

            T0 = Turn(l, 0)
            values(T0, 0)
            for v in range(LEAD):
                pool_max_parts(pool, l, T0, v)

            def body(T, first, last):
                for j in range(TURN):
                    if j % NC == 1 and not (last and slot(j) == 1):
                        if not (first and slot(j) == 0):
                            pool.wait_ge(asem(l, "weighed"), T.steps(slot(j) * STEPS[l]))
                        values(T, slot(j) + 1)
                    if ahead(l, j, last):
                        pool_max_parts(pool, l, T, j + LEAD)

            turns(pool, l, body, pool_chain, TURN * PART_LINKS)

        def sp_operands(sp, l, head, s):
            for a in range(PARTS):
                rows = slice(a * PARTS * HD, (a + 1) * PARTS * HD)
                q = bass.AP(QD[l].tensor, head * (HD * N) + a * P * N, [[0, PARTS], [N, HD], [1, N]])
                k = bass.AP(KD[l].tensor, head * (HD * N), [[P * N, PARTS], [N, HD], [1, N]])
                sp.dma_start(QS[s][rows, :], q).then_inc(asem(l, "operands"), 16)
                sp.dma_start(KS[s][rows, :], k).then_inc(asem(l, "operands"), 16)

        def sp_max_rows(sp, l, T, v):
            c = chunk(l, v)
            sp.wait_ge(asem(l, "max_row_copied"), T.units(v + 1))
            dst = QS[slot(v)][SHIFT_ROW:SHIFT_ROW + PARTS, c * C:(c + 1) * C].rearrange("p (t n) -> p t n", t=TC)
            sp.dma_start(dst, max_row[0:PARTS * TC, v % 4, :]).then_inc(asem(l, f"max_shift{v % 2}_"), 16)

        def sp_attention(sp, l):
            sp.wait_ge(sem(f"parts_stored{l}"), 2 * NC * 16)
            sp_operands(sp, l, 0, 0)
            for v in range(ROWS_AHEAD[l]):
                sp_max_rows(sp, l, Turn(l, 0), v)

            def body(T, first, last):
                for j in range(TURN):
                    if j % NC == 0 and not (last and slot(j) == 1):
                        if not (first and slot(j) == 0):
                            sp.wait_ge(asem(l, "weighed"), T.steps(slot(j) * STEPS[l]))
                        sp_operands(sp, l, T.heads(slot(j) + 1), (slot(j) + 1) % 2)
                    for _, v in row_events(l, j, last):
                        sp_max_rows(sp, l, T, v)

            turns(sp, l, body)

        def dve_front(dve, l):
            dve.sem_inc(sem(f"parts_ready{l}"), 1)
            with loop(dve, [link_chain, var_chain, std_chain], [3, 1, 1]) as c:
                dve_norm(dve, lambda t: tile_of(X, c, t))
                for t in range(TC):
                    ins = dve_scale(tile_of(XN, c, t), tile_of(X, c, t), t)
                ins.then_inc(sem(f"xn_ready{l}"), 1)
            with loop(dve, [link_chain], [6]) as c:
                for i, parts in ((0, QP), (1, KP)):
                    dve.wait_ge(sem(f"qk_biased{l}"), c * 2 + (i + 1))
                    p = [parts[:, a, cols(c)] for a in range(PARTS)]
                    dve_link(dve, nc.vector.tensor_copy(p[0], QF[i]))
                    dve_link(dve, nc.vector.tensor_tensor(QR[i], QF[i], p[0], ALU.subtract))
                    dve_link(dve, nc.vector.tensor_copy(p[1], QR[i]))
                    nc.vector.tensor_tensor(p[2], QR[i], p[1], ALU.subtract).then_inc(sem(f"parts_ready{l}"), 1)
                dve.wait_ge(sem(f"v_ready{l}"), c + 1)
                dst = V[:, bass.ds(c * TC, TC), :, 0:HD]
                src = bank(3).rearrange("p (t h d) -> p t h d", t=TC, h=H)
                if l == 0:
                    ins = nc.vector.tensor_copy(dst, src)
                else:
                    b = bias_bc[:, 1, :].rearrange("p (h d) -> p h d", h=H).unsqueeze(1).broadcast_to((P, TC, H, HD))
                    ins = nc.vector.tensor_tensor(dst, src, b, ALU.add)
                ins.then_inc(sem(f"v_taken{l}"), 1)

        def pe_transposes(src, b):
            for t in range(TC):
                ins = nc.tensor.transpose(PS[:, b * C + t * P:b * C + (t + 1) * P], src(t), ident[:, :])
            return ins

        def pe_front(pe, l):
            for c in range(NC):
                pe.wait_ge(sem(f"xn_ready{l}"), c + 1)
                pe.wait_ge(sem(f"xt_ready{l}"), c)
                pe_transposes(lambda t: tile_of(XN, c, t), 0).then_inc(sem(f"x_transposed{l}"), 1)
                pe.wait_ge(sem(f"xt_ready{l}"), c + 1)
                for i, w in ((0, W_Q[l]), (1, W_K[l])):
                    pe.wait_ge(sem(f"qk_biased{l}"), c * 2)
                    nc.tensor.matmul(bank(1 + i), WT[:, w, :], XT[:, cols(c)], start=True, stop=True)\
                        .then_inc(sem(f"qk_ready{l}"), 1)
                pe.wait_ge(sem(f"v_taken{l}"), c)
                for t in range(TC):
                    ins = nc.tensor.matmul(PS[:, 3 * C + t * P:3 * C + (t + 1) * P], XT[:, cols(c, t, P)],
                                           WT[:, W_V[l], :], start=True, stop=True)
                ins.then_inc(sem(f"v_ready{l}"), 1)

        def act_front(act, l):
            with loop(act, act_norms, [1, 1]) as c:
                act_std(act)
            with act.Fori(0, NC) as c:
                act.wait_ge(sem(f"x_transposed{l}"), c + 1)
                nc.scalar.copy(XT[:, cols(c)], bank(0)).then_inc(sem(f"xt_ready{l}"), 1)
                for i in range(2):
                    act.wait_ge(sem(f"qk_ready{l}"), c * 2 + (i + 1))
                    act.wait_ge(sem(f"parts_ready{l}"), c * 2 + 1)
                    if l == 0:
                        ins = nc.scalar.copy(QF[i], bank(1 + i))
                    else:
                        ins = nc.scalar.activation(QF[i], bank(1 + i), ACT.Identity, bias=bias_qk[:, i:i + 1])
                    ins.then_inc(sem(f"qk_biased{l}"), 1)

        def sp_front(sp, l):
            with sp.Fori(0, NC) as c:
                for i, (parts, dst) in enumerate(((QP, QD[l]), (KP, KD[l]))):
                    sp.wait_ge(sem(f"parts_ready{l}"), c * 2 + (i + 2))
                    sp.dma_start(dst[:, :, cols(c)].rearrange("a p n -> p a n"), parts[:, :, cols(c)])\
                        .then_inc(sem(f"parts_stored{l}"), 16)

        def pe_project(pe, l):
            pe.wait_ge(asem(l, "o_used"), H * NC)
            for c in range(NC):
                pe.wait_ge(sem(f"ot_ready{l}"), c)
                pe_transposes(lambda t: tile_of(ON, c, t), 0).then_inc(sem(f"ot_transposed{l}"), 1)
                pe.wait_ge(sem(f"ot_ready{l}"), c + 1)
                pe.wait_ge(sem(f"y_taken{l}"), c)
                for t in range(TC):
                    ins = nc.tensor.matmul(PS[:, C + t * P:C + (t + 1) * P], XT[:, cols(c, t, P)],
                                           WT[:, W_O[l], :], start=True, stop=True)
                ins.then_inc(sem(f"y_ready{l}"), 1)

        def act_project(act, l):
            with loop(act, act_norms, [1, 1]) as c:
                act.wait_ge(sem(f"ot_transposed{l}"), c + 1)
                nc.scalar.copy(XT[:, cols(c)], bank(0)).then_inc(sem(f"ot_ready{l}"), 1)
                act_std(act)

        def dve_project(dve, l):
            bias = bias_bc[:, 0 if l == 0 else 2, :].unsqueeze(1).broadcast_to((P, TC, P))
            with loop(dve, [link_chain, var_chain, std_chain], [5, 1, 1]) as c:
                dve.wait_ge(sem(f"y_ready{l}"), c + 1)
                ins = nc.vector.tensor_tensor(chunk_of(XN, c), bank(1).rearrange("p (t n) -> p t n", t=TC), bias,
                                              ALU.add)
                ins.then_inc(sem(f"y_taken{l}"), 1)
                dve.wait_ge(sem(f"y_taken{l}"), c + 1)
                dve_norm(dve, lambda t: tile_of(XN, c, t))
                dve_residual(dve, c)

        def dve_residual(dve, c):
            for t in range(TC):
                ins = dve_scale(tile_of(XN, c, t), tile_of(XN, c, t), t)
            dve_link(dve, ins)
            dve_link(dve, nc.vector.tensor_tensor(chunk_of(X, c), chunk_of(X, c), chunk_of(XN, c), ALU.add))

        def dve_pick(dve):
            with loop(dve, [link_chain, var_chain, std_chain], [3, 1, 1]) as c:
                dve_norm(dve, lambda t: tile_of(X, c, t))
                for t in range(TC):
                    ins = dve_scale(tile_of(XN, c, t), tile_of(X, c, t), t)
                ins.then_inc(sem("pick_xn"), 1)
            with loop(dve, [link_chain, var_chain, std_chain], [4 + 2 * TC + 5, 1, 1]) as c:
                dve.wait_ge(sem("pick_scores"), c + 1)
                s = bank(1)[:, 0:TC * NE].rearrange("p (t e) -> p t e", t=TC)

                def bc(v):
                    return v.unsqueeze(2).broadcast_to((P, TC, NE))

                dve_link(dve, nc.vector.tensor_reduce(sc_max[:, :], s, AX.X, ALU.max))
                dve_link(dve, nc.vector.tensor_tensor(sc_hit[:, :, :], s, bc(sc_max[:, :]), ALU.is_equal))
                nc.vector.tensor_tensor(sc_hit[:, :, :], sc_hit[:, :, :], tie[:, :, :], ALU.mult)\
                    .then_inc(sem("pick_hit"), 1)
                dve.wait_ge(sem("pick_hit"), c + 1)
                dve_link(dve, nc.vector.tensor_reduce(sc_max[:, :], sc_hit[:, :, :], AX.X, ALU.max))
                dve_link(dve, nc.vector.tensor_tensor(onehot[:, :, :], sc_hit[:, :, :], bc(sc_max[:, :]), ALU.is_equal))
                for t in range(TC):
                    dve.wait_ge(sem("pick_experts"), c * TC + (t + 1))
                    b = bank(2 + 2 * (t % 2), 2).rearrange("p (e f) -> p e f", e=NE)
                    oh = onehot[:, t, :].unsqueeze(2).broadcast_to((P, NE, P))
                    nc.vector.tensor_tensor(picked, b, oh, ALU.mult).then_inc(sem("pick_taken"), 1)
                    dve.wait_ge(sem("pick_taken"), c * TC + (t + 1))
                    dve_link(dve, nc.vector.tensor_reduce(QF[0][:, 0:P], picked.rearrange("p e f -> p f e"), AX.X,
                                                          ALU.add))
                    x = tile_of(XN, c, t)
                    dve_link(dve, nc.vector.tensor_tensor(x, x, QF[0][:, 0:P], ALU.add))
                dve_norm(dve, lambda t: tile_of(XN, c, t))
                dve_residual(dve, c)

        def pe_pick(pe):
            for c in range(NC):
                pe.wait_ge(sem("pick_xn"), c + 1)
                pe.wait_ge(sem("pick_xt"), c)
                pe_transposes(lambda t: tile_of(XN, c, t), 0).then_inc(sem("pick_transposed"), 1)
                pe.wait_ge(sem("pick_xt"), c + 1)
                pe.wait_ge(sem("pick_hit"), c)
                for t in range(TC):
                    ins = nc.tensor.matmul(PS[:, C + t * NE:C + (t + 1) * NE], XT[:, cols(c, t, P)], gateT[:, :],
                                           start=True, stop=True)
                ins.then_inc(sem("pick_scores"), 1)
                for t in range(TC):
                    if t >= 2:
                        pe.wait_ge(sem("pick_taken"), c * TC + (t - 1))
                    else:
                        pe.wait_ge(sem("pick_taken"), c * TC)
                    for i in range(2):
                        w = WT[:, W_E + 4 * i:W_E + 4 * (i + 1), :].rearrange("p e f -> p (e f)")
                        ins = nc.tensor.matmul(bank(2 + 2 * (t % 2) + i), XT[:, cols(c, t, P)], w, start=True, stop=True)
                    ins.then_inc(sem("pick_experts"), 1)

        def act_pick(act):
            with loop(act, act_norms, [1, 1]) as c:
                act_std(act)
            with loop(act, act_norms, [1, 1]) as c:
                act.wait_ge(sem("pick_transposed"), c + 1)
                nc.scalar.copy(XT[:, cols(c)], bank(0)).then_inc(sem("pick_xt"), 1)
                act_std(act)

        def dve_mix(dve):
            for name in ("mix_xc", "mix_h", "mix_got"):
                dve.sem_inc(sem(name), 1)
            with loop(dve, [link_chain, var_chain, std_chain], [3, 1, 1]) as c:
                dve_norm(dve, lambda t: tile_of(X, c, t))
                for t in range(TC):
                    ins = dve_scale(tile_of(XN, c, t), tile_of(X, c, t), t)
                ins.then_inc(sem("mix_xn"), 1)
            dve.wait_ge(sem("mix_logits"), NC)

            def bc(v):
                return v.unsqueeze(3).broadcast_to((P, NT, 2, NE))

            lg = bank(1)[:, 0:NT * 2 * NE].rearrange("p (t k e) -> p t k e", t=NT, k=2)
            dve_link(dve, nc.vector.tensor_reduce(lred[:, :, :], lg, AX.X, ALU.max))
            nc.vector.tensor_tensor(logit[:, :, :, :], lg, bc(lred[:, :, :]), ALU.subtract).then_inc(sem("mix_shifted"), 1)
            dve.wait_ge(sem("mix_exp"), 2)
            dve_link(dve, nc.vector.tensor_reduce(lred[:, :, :], expo[:, :, :, :], AX.X, ALU.add))
            dve_link(dve, nc.vector.reciprocal(linv[:, :, :], lred[:, :, :]))
            dve_link(dve, nc.vector.tensor_tensor(logit[:, :, :, :], expo[:, :, :, :], bc(linv[:, :, :]), ALU.mult))
            dve_link(dve, nc.vector.tensor_tensor(cw[:, :, :], logit[:, :, 0, :], logit[:, :, 1, :], ALU.mult))
            dve_link(dve, nc.vector.tensor_reduce(lred[:, :, 0], cw[:, :, :], AX.X, ALU.add))
            dve_link(dve, nc.vector.tensor_scalar(linv[:, :, 0], lred[:, :, 0], 1e-9, None, ALU.add))
            dve_link(dve, nc.vector.reciprocal(lred[:, :, 1], linv[:, :, 0]))
            nc.vector.tensor_tensor(cw[:, :, :], cw[:, :, :], lred[:, :, 1].unsqueeze(2).broadcast_to((P, NT, NE)),
                                    ALU.mult).then_inc(sem("mix_cw"), 1)
            with dve.Fori(0, NC // 2) as cc:
                link_chain.enter(cc, 8)
                var_chain.enter(cc, 2)
                std_chain.enter(cc, 2)
                for k in range(2):
                    dve_mix_chunk(dve, cc, k)
            for ch in (link_chain, var_chain, std_chain):
                ch.leave(NC // 2)

        def dve_mix_chunk(dve, cc, k):
            c = cc * 2 + k

            def weighted(e):
                if e == 0:
                    dve.wait_ge(sem(f"cw_loaded{k}"), cc * 16 + 16)
                if e >= 2:
                    dve.wait_ge(sem("mix_u"), c * 32 + (4 * e - 3))
                else:
                    dve.wait_ge(sem("mix_u"), c * 32 + 1)
                nc.vector.tensor_tensor(XC[e % 2], XT[:, cols(c)], CWB[k][:, e, :], ALU.mult).then_inc(sem("mix_xc"), 1)

            weighted(0)
            for i in range(32):
                if i % FB == 0 and i // FB + 1 < NE:
                    weighted(i // FB + 1)
                dve.wait_ge(sem("mix_silu"), c * 32 + (i + 2))
                dve.wait_ge(sem("mix_u"), c * 32 + (i + 2))
                if i >= 4:
                    dve.wait_ge(sem("mix_down"), c * 32 + (i - 3))
                nc.vector.tensor_tensor(HB[i % 4], SG[i % 4], bank(4 + i % 2), ALU.mult).then_inc(sem("mix_h"), 1)
            dve.wait_ge(sem("mix_back"), c + 1)
            nc.vector.tensor_copy(chunk_of(XN, c), bank(0).rearrange("p (t n) -> p t n", t=TC)).then_inc(sem("mix_got"), 1)
            dve.wait_ge(sem("mix_got"), c + 2)
            dve_norm(dve, lambda t: tile_of(XN, c, t))
            for t in range(TC):
                ins = dve_scale(tile_of(XN, c, t), tile_of(XN, c, t), t)
            dve_link(dve, ins)
            nc.vector.tensor_tensor(chunk_of(X, c), chunk_of(X, c), chunk_of(XN, c), ALU.add).then_inc(sem("x_final"), 1)

        def act_mix(act):
            for name in ("mix_silu", "mix_out"):
                act.sem_inc(sem(name), 1)
            with loop(act, act_norms, [1, 1]) as c:
                act_std(act)
            with act.Fori(0, NC) as c:
                act.wait_ge(sem("mix_transposed"), c + 1)
                nc.scalar.copy(XT[:, cols(c)], bank(0)).then_inc(sem("mix_xt"), 1)
            act.wait_ge(sem("mix_shifted"), 1)
            nc.scalar.activation(expo[:, :, 0, :], logit[:, :, 0, :], ACT.Exp).then_inc(sem("mix_exp"), 1)
            nc.scalar.activation(expo[:, :, 1, :], logit[:, :, 1, :], ACT.Exp, scale=1.0 / GATE_TEMP)\
                .then_inc(sem("mix_exp"), 1)
            act.wait_ge(sem("cw_transposed"), 1)
            nc.scalar.copy(cwT[:, :], bank(0)[:, 0:P]).then_inc(sem("cw_rows"), 1)
            with loop(act, act_norms, [1, 1]) as c:
                for i in range(32):
                    act.wait_ge(sem("mix_g"), c * 32 + (i + 1))
                    if i >= 4:
                        act.wait_ge(sem("mix_h"), c * 32 + (i - 2))
                    nc.scalar.activation(SG[i % 4], bank(2 + i % 2), ACT.Silu).then_inc(sem("mix_silu"), 1)
                act.wait_ge(sem("mix_down"), c * 32 + 32)
                nc.scalar.copy(o_sb[:, 0, :], bank(6)).then_inc(sem("mix_out"), 1)
                act_std(act)

        def pe_mix(pe):
            pe.sem_inc(sem("mix_u"), 1)
            for c in range(NC):
                pe.wait_ge(sem("mix_xn"), c + 1)
                pe.wait_ge(sem("mix_xt"), c)
                pe_transposes(lambda t: tile_of(XN, c, t), 0).then_inc(sem("mix_transposed"), 1)
                pe.wait_ge(sem("mix_xt"), c + 1)
                for t in range(TC):
                    ins = nc.tensor.matmul(PS[:, bass.ds(c * (TC * 2 * NE) + (C + t * 2 * NE), 2 * NE)],
                                           XT[:, cols(c, t, P)], rgw[:, :, :].rearrange("p k e -> p (k e)"),
                                           start=True, stop=True)
                ins.then_inc(sem("mix_logits"), 1)
            pe.wait_ge(sem("mix_cw"), 1)
            nc.tensor.transpose(bank(0)[:, 0:P], cw[:, :, :].rearrange("p t e -> p (t e)"), ident[:, :])\
                .then_inc(sem("cw_transposed"), 1)
            with pe.Fori(0, NC) as c:
                def down(i):
                    pe.wait_ge(sem("mix_h"), c * 32 + (i + 2))
                    if i == 0:
                        pe.wait_ge(sem("mix_out"), c + 1)
                        pe.wait_ge(sem("wd_loaded"), 16)
                    nc.tensor.matmul(bank(6), Wd[:, i, :], HB[i % 4], start=i == 0, stop=i == 31)\
                        .then_inc(sem("mix_down"), 1)

                for i in range(32):
                    e, f = divmod(i, FB)
                    pe.wait_ge(sem("mix_silu"), c * 32 + max(i, 1))
                    nc.tensor.matmul(bank(2 + i % 2), Wg[:, e, f * P:(f + 1) * P], XT[:, cols(c)], start=True, stop=True)\
                        .then_inc(sem("mix_g"), 1)
                    pe.wait_ge(sem("mix_h"), c * 32 + max(i, 1))
                    if f == 0:
                        pe.wait_ge(sem("mix_xc"), c * NE + (e + 2))
                    nc.tensor.matmul(bank(4 + i % 2), Wu[:, e, f * P:(f + 1) * P], XC[e % 2], start=True, stop=True)\
                        .then_inc(sem("mix_u"), 1)
                    if i >= 1:
                        down(i - 1)
                down(31)
                pe.wait_ge(sem("mix_out"), c + 2)
                pe.wait_ge(sem("cw_rows"), 1)
                pe.wait_ge(sem("mix_got"), c + 1)
                pe_transposes(lambda t: o_sb[:, 0, t * P:(t + 1) * P], 0).then_inc(sem("mix_back"), 1)

        def sp_mix(sp):
            sp.wait_ge(sem("x_transposed1"), NC)
            sp.wait_ge(asem(1, "o_used"), H * NC)
            sp.dma_start(Wd[:, :, :], w_down.rearrange("e (f p) h -> p (e f) h", p=P)).then_inc(sem("wd_loaded"), 16)
            sp.wait_ge(sem("cw_rows"), 1)
            for t in range(NT):
                sp.dma_start(CD[:, t * P:(t + 1) * P], cwT[t * NE:(t + 1) * NE, :]).then_inc(sem("cw_stored"), 16)
            sp.wait_ge(sem("cw_stored"), NT * 16)
            out_v = out[0].rearrange("(t p) d -> p t d", p=P)

            def load(c):
                if c >= 2:
                    sp.wait_ge(sem("mix_xc"), 1 + (c - 1) * NE)
                src = bass.AP(CD.tensor, c * C, [[0, P], [N, NE], [1, C]])
                sp.dma_start(CWB[c % 2], src).then_inc(sem(f"cw_loaded{c % 2}"), 16)

            load(0)
            load(1)
            for c in range(NC):
                if c + 2 < NC:
                    load(c + 2)
                sp.wait_ge(sem("x_final"), c + 1)
                sp.dma_start(out_v[:, c * TC:(c + 1) * TC, :], chunk_of(X, c)).then_inc(sem("stored"), 16)
            sp.wait_ge(sem("stored"), NC * 16)

        CONSTS, PADS = 4 + NE, 5
        block = ctx.enter_context(nc.Block())

        @block.sync
        def _(sp):
            sp.dma_start(X[:, :, :], x_in[0].rearrange("(t p) d -> p t d", p=P)).then_inc(sem("x_loaded"), 16)
            sp.dma_start(raw[:, 0:3, :], w_qkv.rearrange("(b p) c -> p b c", p=P)).then_inc(sem("w_loaded"), 16)
            for i, w in ((3, w_proj), (4, Wq), (5, Wk), (6, Wv), (7, Wo)):
                sp.dma_start(raw[:, i, :], w).then_inc(sem("w_loaded"), 16)
            sp.dma_start(raw[:, W_E:W_E + NE, :], expert_w.rearrange("e f h -> f e h")).then_inc(sem("w_loaded"), 16)
            sp.dma_start(raw_gate, gate_w).then_inc(sem("w_loaded"), 16)
            for i, b in enumerate((b_proj, bv, bo)):
                sp.dma_start(bias_bc[:, i, :], b.partition_broadcast(P)).then_inc(sem("b_loaded"), 16)
            for i, b in enumerate((bq, bk)):
                sp.dma_start(bias_qk[:, i:i + 1], b.rearrange("(p a) -> p a", a=1)).then_inc(sem("b_loaded"), 16)
            for i, w in enumerate((w_router, w_gating)):
                sp.dma_start(rgw[:, i, :], w).then_inc(sem("b_loaded"), 16)
            sp.dma_start(Wg[:, :, :], w_gate.rearrange("e h f -> h e f")).then_inc(sem("wgu_loaded"), 16)
            sp.dma_start(Wu[:, :, :], w_up.rearrange("e h f -> h e f")).then_inc(sem("wgu_loaded"), 16)
            sp_front(sp, 0)
            sp_attention(sp, 0)
            sp_front(sp, 1)
            sp_attention(sp, 1)
            sp_mix(sp)

        @block.gpsimd
        def _(pool):
            nc.gpsimd.memset(ident[:, :], 0.0).then_inc(sem("zeroed"), 1)
            nc.gpsimd.memset(identb[:, :], 0.0).then_inc(sem("zeroed"), 1)
            nc.gpsimd.memset(mask_nat[:, :], 0.0).then_inc(sem("zeroed"), 1)
            nc.gpsimd.memset(mask_t[:, :], 0.0).then_inc(sem("zeroed"), 1)
            nc.gpsimd.memset(zeros[:, :], 0.0).then_inc(sem("zeroed"), 1)
            pool.wait_ge(sem("zeroed"), 5)
            for m in (ident, identb):
                nc.gpsimd.affine_select(out=m[:, :], in_=m[:, :], compare_op=ALU.not_equal, fill=1.0, base=0,
                                        pattern=[[-1, P]], channel_multiplier=1).then_inc(sem("consts"), 1)
            nc.gpsimd.affine_select(out=mask_nat[:, :], in_=mask_nat[:, :], compare_op=ALU.is_ge, fill=MASKED, base=0,
                                    pattern=[[-1, P]], channel_multiplier=1).then_inc(sem("consts"), 1)
            nc.gpsimd.affine_select(out=mask_t[:, :], in_=mask_t[:, :], compare_op=ALU.is_ge, fill=MASKED, base=0,
                                    pattern=[[1, P]], channel_multiplier=-1).then_inc(sem("consts"), 1)
            for e in range(NE):
                nc.gpsimd.memset(tie[:, :, e], float(NE - e)).then_inc(sem("consts"), 1)
            for s in range(2):
                nc.gpsimd.memset(VH[s], 0.0).then_inc(sem("v_zeroed"), 1)
                pool.wait_ge(sem("v_zeroed"), s + 1)
                nc.gpsimd.memset(VH[s][:, :, HD], 1.0).then_inc(sem("pads"), 1)
                nc.gpsimd.memset(QS[s], 0.0).then_inc(sem("pads"), 1)
                nc.gpsimd.memset(KS[s], 0.0).then_inc(sem("ks_zeroed"), 1)
                pool.wait_ge(sem("ks_zeroed"), s + 1)
                nc.gpsimd.memset(KS[s][SHIFT_ROW:P, :], 1.0).then_inc(sem("ks_ones"), 1)
                pool.wait_ge(sem("ks_ones"), s + 1)
            nc.gpsimd.memset(probs_diag[:, :, :], 0.0).then_inc(sem("pads"), 1)
            pool.wait_ge(sem("pads"), PADS)
            pool_attention(pool, 0)
            pool_attention(pool, 1)

        @block.scalar
        def _(act):
            for b in range(4):
                act.wait_ge(sem("w_transposed"), b + 1)
                nc.scalar.copy(WT[:, 4 * b:4 * b + 4, :].rearrange("p b c -> p (b c)"), bank(b + 1))\
                    .then_inc(sem("w_ready"), 1)
            act.wait_ge(sem("w_transposed"), 5)
            nc.scalar.copy(gateT[:, :], bank(5)[:, 0:NE]).then_inc(sem("w_ready"), 1)
            act.wait_ge(sem("b_loaded"), 7 * 16)
            act_front(act, 0)
            act.wait_ge(sem("pads"), PADS)
            act_attention(act, 0)
            act_project(act, 0)
            act_pick(act)
            act_front(act, 1)
            act_attention(act, 1)
            act_project(act, 1)
            act_mix(act)

        @block.vector
        def _(dve):
            nc.vector.memset(held[:, :], 0.0).then_inc(sem("held_ready"), 1)
            dve.wait_ge(sem("held_ready"), 1)
            dve.wait_ge(sem("x_loaded"), 16)
            dve.wait_ge(sem("b_loaded"), 7 * 16)
            dve.wait_ge(sem("consts"), CONSTS)
            dve.wait_ge(sem("pads"), PADS)
            dve_front(dve, 0)
            dve_attention(dve, 0)
            dve_project(dve, 0)
            dve_pick(dve)
            dve_front(dve, 1)
            dve_attention(dve, 1)
            dve_project(dve, 1)
            dve_mix(dve)

        @block.tensor
        def _(pe):
            pe.wait_ge(sem("consts"), CONSTS)
            pe.wait_ge(sem("w_loaded"), 8 * 16)
            for b in range(4):
                for i in range(4):
                    ins = nc.tensor.transpose(PS[:, (b + 1) * C + i * P:(b + 1) * C + (i + 1) * P], raw[:, 4 * b + i, :],
                                              ident[:, :])
                ins.then_inc(sem("w_transposed"), 1)
            nc.tensor.transpose(bank(5)[:, 0:NE], raw_gate, ident[0:NE, 0:NE]).then_inc(sem("w_transposed"), 1)
            pe.wait_ge(sem("w_ready"), 5)
            pe.wait_ge(sem("b_loaded"), 7 * 16)
            pe.wait_ge(sem("pads"), PADS)
            pe.wait_ge(sem("wgu_loaded"), 32)
            pe_front(pe, 0)
            pe_attention(pe, 0)
            pe_project(pe, 0)
            pe_pick(pe)
            pe_front(pe, 1)
            pe_attention(pe, 1)
            pe_project(pe, 1)
            pe_mix(pe)


INS = ['L0_attn_x', 'L0_attn_w_qkv', 'L0_attn_w_proj', 'L0_attn_b_proj', 'L0_ffn_gate_w', 'L0_ffn_expert_w',
       'L1_attn_Wq', 'L1_attn_bq', 'L1_attn_Wk', 'L1_attn_bk', 'L1_attn_Wv', 'L1_attn_bv', 'L1_attn_Wo', 'L1_attn_bo',
       'L1_ffn_w_router', 'L1_ffn_w_gating', 'L1_ffn_w_gate', 'L1_ffn_w_up', 'L1_ffn_w_down']


def kernel(**inputs):
    import numpy as np
    import concourse.bacc as bacc
    from concourse.bass_utils import run_bass_kernel_spmd

    nc = bacc.Bacc("TRN2", target_bir_lowering=False, num_devices=1)
    arrays, args = {}, []
    for name in INS:
        a = np.ascontiguousarray(inputs[name])
        arrays[f"in_{name}"] = a
        args.append(nc.dram_tensor(f"in_{name}", a.shape, mybir.dt.from_np(a.dtype), kind="ExternalInput").ap())
    out = nc.dram_tensor("out", (1, N, P), FP32, kind="ExternalOutput").ap()
    sandwich(nc, *args, out)
    r = run_bass_kernel_spmd(nc, [arrays], core_ids=[0])
    return r.results[0]["out"]
```

```python
import concourse.bass as bass
from concourse import mybir
from contextlib import ExitStack

FP32 = mybir.dt.float32
BF16 = mybir.dt.bfloat16
ALU = mybir.AluOpType
ACT = mybir.ActivationFunctionType
AX = mybir.AxisListType

P = 128
N = 2048
NT = N // P
C = 512
NC = N // C
TC = C // P
H = 16
HD = P // H
SCALE = HD ** -0.5
NE = 8
F = 512
FB = F // P
LN_EPS = 1e-5
MASKED = -9e15
GATE_TEMP = 0.1

PARTS = 3
ROWS = PARTS * PARTS * HD
NAT_ROWS = 96
SHIFT_ROW = 96
T_ROWS = SHIFT_ROW + PARTS


class Chain:

    def __init__(self, sem):
        self.sem, self.n, self.turn, self.per, self.start = sem, 0, None, 0, 0

    def enter(self, turn, per):
        self.turn, self.per, self.start = turn, per, self.n

    def leave(self, turns):
        assert self.n - self.start == self.per, (self.n - self.start, self.per)
        self.n, self.turn = self.start + self.per * turns, None

    def value(self):
        return self.n if self.turn is None else self.turn * self.per + self.n


def sandwich(nc, x_in, w_qkv, w_proj, b_proj, gate_w, expert_w, Wq, bq, Wk, bk, Wv, bv, Wo, bo,
             w_router, w_gating, w_gate, w_up, w_down, out):
    ctx = ExitStack()
    with ctx:
        def sb(name, shape, dt=FP32):
            return ctx.enter_context(nc.sbuf_tensor(name, shape, dt))

        sems = {}

        def sem(name):
            if name not in sems:
                sems[name] = ctx.enter_context(nc.semaphore(name))
            return sems[name]

        X = sb("X", [P, NT, P])
        XN = sb("XN", [P, NT, P])
        XT = sb("XT", [P, N])
        ON = sb("ON", [P, NT, P])
        ident = sb("ident", [P, P])
        identb = sb("identb", [P, P], BF16)
        mask_nat = sb("mask_nat", [P, P], BF16)
        mask_t = sb("mask_t", [P, P], BF16)
        WT = sb("WT", [P, 16, P])
        gateT = sb("gateT", [P, NE])
        rgw = sb("rgw", [P, 2, NE])
        bias_bc = sb("bias_bc", [P, 3, P])
        bias_qk = sb("bias_qk", [P, 2])
        Wg = sb("Wg", [P, NE, F])
        Wu = sb("Wu", [P, NE, F])
        probs_diag = sb("probs_diag", [P, 2, TC, C])
        o_sb = sb("o_sb", [P, 2, C])
        max_row = sb("max_row", [P, 4, P], BF16)
        stats = sb("stats", [P, TC, 6])
        held = sb("held", [P, 2])
        mv = sb("mv", [P, NC, TC, 2])
        var_eps = sb("var_eps", [P, NC, TC])
        std = sb("std", [P, NC, TC])
        rstd = sb("rstd", [P, NC, TC])
        mx = sb("mx", [P, 4, TC, 2])
        zeros = sb("zeros", [P, TC])
        neg_max = sb("neg_max", [P, 4, TC])
        rest1 = sb("rest1", [P, TC])
        max_parts = sb("max_parts", [P, 4, PARTS, TC], BF16)
        osum = sb("osum", [P, 2, TC, HD + 1])
        oinv = sb("oinv", [P, 2, TC])
        logit = sb("logit", [P, NT, 2, NE])
        expo = sb("expo", [P, NT, 2, NE])
        lred = sb("lred", [P, NT, 2])
        linv = sb("linv", [P, NT, 2])
        cw = sb("cw", [P, NT, NE])
        cw_by_expert = sb("cw_by_expert", [P, NE, NT])
        cwT = sb("cwT", [P, P])
        tie = sb("tie", [P, TC, NE])
        sc_max = sb("sc_max", [P, TC])
        sc_hit = sb("sc_hit", [P, TC, NE])
        onehot = sb("onehot", [P, NC, TC, NE])
        pick_sum = sb("pick_sum", [P, P])

        A = sb("A", [P, 20480])
        V = A[:, 0:2048].rearrange("p (t h d) -> p t h d", t=NT, h=H)
        VH = [A[:, 2048 + 512 * s:2560 + 512 * s].rearrange("p (t d) -> p t d", t=NT)
              for s in range(2)]
        probs = A[:, 3072:7168].rearrange("p (g t n) -> p g t n", g=2, t=TC)
        QS = [A[:, 8192 + 1024 * s:8192 + 1024 * (s + 1)].bitcast(BF16) for s in range(2)]
        KS = [A[:, 10240 + 1024 * s:10240 + 1024 * (s + 1)].bitcast(BF16) for s in range(2)]
        QP = A[:, 12288:15360].bitcast(BF16).rearrange("p (a n) -> p a n", a=PARTS)
        KP = A[:, 15360:18432].bitcast(BF16).rearrange("p (a n) -> p a n", a=PARTS)
        QF = [A[:, 18432 + C * i:18432 + C * (i + 1)] for i in range(2)]
        QR = [A[:, 19456 + C * i:19456 + C * (i + 1)] for i in range(2)]
        raw = A[:, 3072:5120].rearrange("p (b c) -> p b c", b=16)
        raw_gate = A[0:NE, 5120:5120 + P]
        picked = [A[:, 3072 + NE * P * i:3072 + NE * P * (i + 1)].rearrange("p (e f) -> p e f", e=NE)
                  for i in range(4)]
        CWB = A[:, 0:4096].rearrange("p (e n) -> p e n", e=NE)
        HB = [A[:, 8192 + C * i:8192 + C * (i + 1)] for i in range(4)]
        SG = [A[:, 10240 + C * i:10240 + C * (i + 1)] for i in range(4)]
        XC = [A[:, 12288 + C * i:12288 + C * (i + 1)] for i in range(2)]
        Wd = A[:, 16384:20480].rearrange("p (k h) -> p k h", h=P)

        W_Q, W_K, W_V, W_O = (0, 4), (1, 5), (2, 6), (3, 7)
        W_E = 8

        PS = ctx.enter_context(nc.psum_tensor("PS", [P, 8 * C], FP32))

        def bank(i, n=1):
            return PS[:, i * C:(i + n) * C]

        QD = [nc.dram_tensor(f"q_parts{l}", (PARTS, P, N), BF16, kind="Internal").ap() for l in range(2)]
        KD = [nc.dram_tensor(f"k_parts{l}", (PARTS, P, N), BF16, kind="Internal").ap() for l in range(2)]
        CD = nc.dram_tensor("cw_rows", (NE, N), FP32, kind="Internal").ap()

        link_sem = sem("dve_link")
        link_chain = Chain(link_sem)
        var_chain, std_chain = Chain(sem("var_ready")), Chain(sem("std_ready"))
        act_norms = [Chain(sem("var_ready")), Chain(sem("std_ready"))]

        def dve_link(dve, ins):
            link_chain.n += 1
            ins.then_inc(link_chain.sem, 1)
            dve.wait_ge(link_chain.sem, link_chain.value())

        def hold_wait():
            nc.vector.tensor_copy(held[:, 1:2], held[:, 0:1])

        def dve_moments(dve, src, c):
            hold_wait()
            for t in range(TC):
                ins = nc.vector.bn_stats(stats[:, t, :], src(t))
            dve_link(dve, ins)
            hold_wait()
            for t in range(TC):
                ins = nc.vector.bn_aggr(mv[:, c, t, :], stats[:, t, :])
            dve_link(dve, ins)
            var_chain.n += 1
            nc.vector.tensor_scalar(var_eps[:, c, :], mv[:, c, :, 1], LN_EPS, None, ALU.add).then_inc(var_chain.sem, 1)

        def dve_inverse_std(dve, c, moments=None):
            if moments is None:
                std_chain.n += 1
                dve.wait_ge(std_chain.sem, std_chain.value())
            else:
                dve.wait_ge(std_chain.sem, moments)
            dve_link(dve, nc.vector.reciprocal(rstd[:, c, :], std[:, c, :]))

        def dve_scale(dst, src, c, t):
            return nc.vector.tensor_scalar(dst, src, mv[:, c, t, 0:1], rstd[:, c, t:t + 1],
                                           ALU.subtract, ALU.mult)

        def act_std(act, c):
            v, s = act_norms
            v.n += 1
            s.n += 1
            act.wait_ge(v.sem, v.value())
            nc.scalar.activation(std[:, c, :], var_eps[:, c, :], ACT.Sqrt).then_inc(s.sem, 1)

        def tile_of(buf, c, t):
            return buf[:, c * TC + t, :]

        def chunk_of(buf, c):
            return buf[:, bass.ds(c * TC, TC), :]

        def cols(c, t=0, n=C):
            return bass.ds(c * C + t * P, n)

        ORDER = [[0, 1, 2, 3], [3, 2, 1, 0]]
        TURN = 2 * NC
        OPERANDS = 2 * PARTS * 16

        def chunk(l, j):
            return ORDER[l][j % NC]

        def key_tiles(l, j):
            return NT if l == 0 else TC * (chunk(l, j) + 1)

        def steps_before(l, j):
            return sum(key_tiles(l, u) for u in range(j))

        def max_items(l, j):
            items, c = [], chunk(l, j)
            for t in range(TC):
                n = N if l == 0 else (TC * c + t + 1) * P
                for s, k0 in enumerate(range(0, n, 2 * C)):
                    pieces = []
                    for k in range(k0, min(k0 + 2 * C, n), C):
                        w = min(C, n - k)
                        pieces.append((k, w, l == 1 and k + w == n))
                    items.append((t, s, pieces))
            return items

        def items_before(l, j):
            return sum(len(max_items(l, u)) for u in range(j))

        def slots(l, j):
            return 2 if l == 0 or chunk(l, j) >= 2 else 1

        BESIDE = [[[[(2, 2 * m, 2 * m + 2)] for m in range(4)]] * NC,
                  [[[(2, 2, 4)], [(3, 0, 4)], [(4, 0, 3)], [(4, 3, 5)]],
                   [[(3, 5, 7)], [(3, 7, 8), (4, 0, 2)], [(4, 2, 4)]],
                   [[(3, 4, 6)], [(3, 6, 8)]],
                   [[(3, 0, 2)]]]]
        BEFORE = [(2, 0), (2, 2)]

        def beside(l, j, m, last):
            return [(j + d, r) for d, a, b in BESIDE[l][j % NC][m] for r in range(a, b)
                    if not (last and j + d >= TURN)]

        def before_all(l):
            whole, more = BEFORE[l]
            return [(v, r) for v in range(whole) for r in range(len(max_items(l, v)))] + \
                [(whole, r) for r in range(more)]

        def is_last_item(l, v, r):
            return r == len(max_items(l, v)) - 1

        def groups(l, j):
            return key_tiles(l, j) // TC

        ITEM_AT = {0: [], 1: [3], 2: [3, 3], 3: [1, 2, 3], 4: [1, 2, 3, 3]}

        OUTPUTS = [[[(1, -1)]] * NC, [[(0, -2), (1, -1)], [(1, -1)], [(1, -1)], []]]

        def outputs(l, j, first):
            return [(m, j + d) for m, d in OUTPUTS[l][j % NC] if not (first and j == 0)]

        def outputs_left(l):
            done = [j + d for j in range(TURN) for _, d in OUTPUTS[l][j % NC]]
            return range(max(done) + 1, TURN)

        def row_events(l, j, last):
            ev = [[[(2, 1)]] * NC, [[(2, 1), (3, 2)], [(0, 2)], [(0, 2)], []]][l][j % NC]
            return [(at, j + d) for at, d in ev if not (last and j + d >= TURN)]

        def row_bank(l, v):
            return 6 + ((v + 1) % 2 if l == 1 and v % NC == 2 else v % 2)

        ROWS_AHEAD = [1, 1]

        STEPS = [steps_before(l, NC) for l in range(2)]
        ITEMS = [items_before(l, NC) for l in range(2)]

        class Turn:

            def __init__(self, l, g):
                self.l, self.g = l, g

            def steps(self, n):
                return self.g * (2 * STEPS[self.l]) + n

            def groups(self, n):
                return self.g * (2 * STEPS[self.l] // TC) + n

            def items(self, n):
                return self.g * (2 * ITEMS[self.l]) + n

            def units(self, n):
                return self.g * TURN + n

            def halves(self, n):
                return self.g * (TURN // 2 * 16) + 16 * n

            def heads(self, n):
                return self.g * 2 + n

        def turns(eng, l, body, chain=None, per=0):
            body(Turn(l, 0), True, False)
            with eng.Fori(1, H // 2 - 1) as g:
                if chain:
                    chain.n -= per
                    chain.enter(g, per)
                body(Turn(l, g), False, False)
            if chain:
                chain.leave(H // 2 - 1)
            body(Turn(l, H // 2 - 1), False, True)

        def asem(l, name):
            return sem(f"{name}{l}")

        def slot(j):
            return j // NC % 2

        def pe_max_item(pe, l, T, v, r):
            c = chunk(l, v)
            t, _, pieces = max_items(l, v)[r]
            r += items_before(l, v)
            if not (isinstance(T.g, int) and T.g == 0 and r < 2):
                pe.wait_ge(asem(l, "max_taken"), T.items(r - 1))
            at = (r % 2) * 2
            q = QS[slot(v)][0:NAT_ROWS, c * C + t * P:c * C + (t + 1) * P]
            for n, (k, w, diag) in enumerate(pieces):
                dst = PS[:, (at + n) * C:(at + n) * C + w]
                ins = nc.tensor.matmul(dst, q, KS[slot(v)][0:NAT_ROWS, k:k + w], start=True, stop=not diag)
                if diag:
                    ins = nc.tensor.matmul(dst[:, w - P:w], identb[:, :], mask_nat[:, :], start=False, stop=True)
            ins.then_inc(asem(l, "max_scores"), 1)

        def row_psum(l, v):
            return PS[0:PARTS * TC, row_bank(l, v) * C:row_bank(l, v) * C + P // 2].bitcast(BF16)

        def pe_max_rows(pe, l, T, v):
            pe.wait_ge(asem(l, "max_parts_ready"), T.units(v + 1))
            nc.tensor.transpose(row_psum(l, v), max_parts[:, v % 4, :, :].rearrange("p a t -> p (a t)"),
                                identb[:, :]).then_inc(asem(l, "max_rows"), 1)

        def pe_transpose_out(pe, l, T, j):
            pe.wait_ge(asem(l, "o_copied"), T.units(j + 1))
            b = (6 + j % 2) * C
            for t in range(TC):
                ins = nc.tensor.transpose(PS[:, b + t * P:b + (t + 1) * P], o_sb[:, j % 2, t * P:(t + 1) * P],
                                          ident[:, :])
            ins.then_inc(asem(l, "o_transposed"), 1)

        def pe_attention(pe, l):
            pe.wait_ge(sem(f"v_taken{l}"), NC)
            pe.wait_ge(asem(l, "operands"), OPERANDS)
            T0 = Turn(l, 0)
            for v, r in before_all(l):
                pe_max_item(pe, l, T0, v, r)
                if is_last_item(l, v, r) and 1 <= v <= ROWS_AHEAD[l]:
                    pe_max_rows(pe, l, T0, v - 1)

            def weigh(T, j, m, last):
                if m == 0:
                    if j % NC == 0:
                        pe.wait_ge(asem(l, "values"), T.heads(slot(j) + 1))
                    if not (isinstance(T.g, int) and T.g == 0 and j < 2):
                        pe.wait_ge(asem(l, "o_used"), T.units(j - 1))
                    for at, v in row_events(l, j, last) if j >= 0 else []:
                        if at == 0:
                            pe.wait_ge(asem(l, "max_row_copied"), T.units(v + 1))
                u = j % TURN
                c, b = chunk(l, u), (6 + u % 2) * C
                diag = l == 1 and m == groups(l, u) - 1
                for t in range(TC):
                    q0 = P * t if diag and c > 0 else 0
                    src = probs_diag[:, u % 2, t, q0:C] if diag else \
                        probs[:, (steps_before(l, u) // TC + m) % 2, t, :]
                    ins = nc.tensor.matmul(PS[32 * t:32 * t + 32, b + q0:b + C], VH[slot(u)][:, TC * m + t, :], src,
                                           start=m == 0, stop=m == groups(l, u) - 1, skip_group_check=True)
                ins.then_inc(asem(l, "weighed"), 1)

            def boundary(T, j, b, first, last):
                for k, (at, v) in enumerate(row_events(l, j, last)):
                    if b == at:
                        if at == 0:
                            if not (first and j < 2):
                                pe.wait_ge(asem(l, "o_used"), T.units(j - 1))
                        elif k:
                            pe.wait_ge(asem(l, "max_row_copied"), T.units(v))
                        elif not (first and j == 0):
                            pe.wait_ge(asem(l, "o_used"), T.units(j))
                        pe_max_rows(pe, l, T, v)

            def scores(T, first, j, i):
                nk, c, n = key_tiles(l, j), chunk(l, j), steps_before(l, j) + i
                if i == 0:
                    pe.wait_ge(asem(l, f"max_shift{j % 2}_"), T.halves(j // 2 + 1))
                if not (first and n < 2):
                    pe.wait_ge(asem(l, "exp_done"), T.steps(n - 1))
                diag = l == 1 and i >= nk - TC
                q0 = P * (i % TC) if diag else 0
                dst = PS[:, (4 + n % 2) * C + q0:(5 + n % 2) * C]
                ins = nc.tensor.matmul(dst, KS[slot(j)][0:T_ROWS, i * P:(i + 1) * P],
                                       QS[slot(j)][0:T_ROWS, c * C + q0:(c + 1) * C], start=True, stop=not diag)
                if diag:
                    ins = nc.tensor.matmul(dst[:, 0:P], identb[:, :], mask_t[:, :], start=False, stop=True)
                ins.then_inc(asem(l, "scores_t"), 1)

            def body(T, first, last):
                behind = None if first else (-1, groups(l, TURN - 1) - 1)
                for j in range(TURN):
                    for m in range(groups(l, j)):
                        items = beside(l, j, m, last)
                        scores(T, first, j, TC * m)
                        scores(T, first, j, TC * m + 1)
                        boundary(T, j, m, first, last)
                        if behind:
                            weigh(T, *behind, last)
                        for at, u in outputs(l, j, first):
                            if m == at:
                                pe_transpose_out(pe, l, T, u)
                        behind = (j, m)
                        for i in (1, 2, 3):
                            if i > 1:
                                scores(T, first, j, TC * m + i)
                            for v, r in [items[k] for k, at in enumerate(ITEM_AT[len(items)]) if at == i]:
                                if v % NC == 0 and r == 0:
                                    pe.wait_ge(asem(l, "operands"), T.heads(v // NC + 1) * OPERANDS)
                                pe_max_item(pe, l, T, v, r)
                    boundary(T, j, groups(l, j), first, last)
                if last:
                    pe.wait_ge(asem(l, "exp_done"), H * STEPS[l])
                    weigh(T, *behind, last)

            turns(pe, l, body)
            for u in outputs_left(l):
                pe_transpose_out(pe, l, Turn(l, H // 2 - 1), u)

        def act_out_copy(act, l, T, j):
            act.wait_ge(asem(l, "weighed"), T.groups(steps_before(l, j + 1) // TC))
            nc.scalar.copy(o_sb[:, j % 2, :], bank(6 + j % 2)).then_inc(asem(l, "o_copied"), 1)

        def act_max_rows(act, l, T, v):
            act.wait_ge(asem(l, "max_rows"), T.units(v + 1))
            nc.scalar.copy(max_row[0:PARTS * TC, v % 4, :], row_psum(l, v)).then_inc(asem(l, "max_row_copied"), 1)

        def act_attention(act, l):
            act.wait_ge(sem(f"parts_stored{l}"), 2 * NC * 16)
            load_operands(act, l, 0, 0, "k")
            for v in range(ROWS_AHEAD[l]):
                act_max_rows(act, l, Turn(l, 0), v)

            def rows_at(T, j, last, i):
                for at, v in row_events(l, j, last):
                    if i == TC * at + (2 if at < groups(l, j) else 0):
                        act_max_rows(act, l, T, v)

            def body(T, first, last):
                for j in range(TURN):
                    nk, n0 = key_tiles(l, j), steps_before(l, j)
                    for i in range(nk):
                        n = n0 + i
                        if i == TC and not (first and j == 0):
                            act_out_copy(act, l, T, j - 1)
                        rows_at(T, j, last, i)
                        act.wait_ge(asem(l, "scores_t"), T.steps(n + 1))
                        diag = l == 1 and i >= nk - TC
                        q0 = P * (i % TC) if diag else 0
                        dst = probs_diag[:, j % 2, i % TC, q0:C] if diag else probs[:, n // TC % 2, i % TC, :]
                        nc.scalar.activation(dst, PS[:, (4 + n % 2) * C + q0:(5 + n % 2) * C], ACT.Exp,
                                             scale=SCALE).then_inc(asem(l, "exp_done"), 1)
                    if nk == TC:
                        act_out_copy(act, l, T, j - 1)
                    rows_at(T, j, last, nk)

            turns(act, l, body)
            act_out_copy(act, l, Turn(l, H // 2 - 1), TURN - 1)

        def dve_reduce(dve, l, T, v, r):
            t, s, pieces = max_items(l, v)[r]
            r += items_before(l, v)
            w = pieces[-1][0] + pieces[-1][1] - pieces[0][0]
            dve.wait_ge(asem(l, "max_scores"), T.items(r + 1))
            at = (r % 2) * 2 * C
            nc.vector.tensor_reduce(mx[:, v % 4, t, s:s + 1], PS[:, at:at + w], AX.X, ALU.max)\
                .then_inc(asem(l, "max_taken"), 1)

        def dve_neg_max(dve, l, T, v):
            dve.wait_ge(asem(l, "max_taken"), T.items(items_before(l, v + 1)))
            nc.vector.tensor_reduce(neg_max[:, v % 4, :], mx[:, v % 4, :, 0:slots(l, v)], AX.X, ALU.max,
                                    negate=True).then_inc(asem(l, "max_known"), 1)

        def dve_output(dve, l, T, j):
            def total():
                dve.wait_ge(asem(l, "o_transposed"), T.units(j + 1))
                src = bank(6 + j % 2).rearrange("p (t g d) -> p t d g", t=TC, g=4)
                nc.vector.tensor_reduce(osum[:, j % 2, :, :], src[:, :, 0:HD + 1, :], AX.X, ALU.add)\
                    .then_inc(asem(l, "o_summed"), 1)

            def inverse():
                dve.wait_ge(asem(l, "o_summed"), T.units(j + 1))
                nc.vector.reciprocal(oinv[:, j % 2, :], osum[:, j % 2, :, HD]).then_inc(asem(l, "o_inverse"), 1)

            def divide():
                dve.wait_ge(asem(l, "o_inverse"), T.units(j + 1))
                c = chunk(l, j)
                dst = ON[:, c * TC:(c + 1) * TC, bass.ds(T.heads(slot(j) if j >= 0 else -1) * HD, HD)]
                nc.vector.tensor_tensor(dst, osum[:, j % 2, :, 0:HD], oinv[:, j % 2, :].unsqueeze(2).broadcast_to((P, TC, HD)),
                                        ALU.mult).then_inc(asem(l, "o_used"), 1)

            return [total, inverse, divide]

        OUT_ITEMS = [[None, [0, 0, 0]], [[0, 0, 0], [0, 1, 1]]]

        def dve_attention(dve, l):
            T0 = Turn(l, 0)
            due = []

            def reduce_item(T, v, r):
                dve_reduce(dve, l, T, v, r)
                if due:
                    dve_neg_max(dve, l, T, due.pop())
                if is_last_item(l, v, r):
                    due.append(v)

            for v, r in before_all(l):
                reduce_item(T0, v, r)

            def body(T, first, last):
                due[:] = [1] if l == 0 else []
                for j in range(TURN):
                    def issued(b):
                        return sum(len(beside(l, j, m, last)) for m in range(b))

                    limit = min([issued(at) for at, _ in row_events(l, j, last) if at > 0] + [issued(groups(l, j))])
                    out_ops = [(issued(m) + k, op) for m, u in outputs(l, j, first)
                               for k, op in zip(OUT_ITEMS[l][m], dve_output(dve, l, T, u))]
                    n = 0
                    for m in range(groups(l, j)):
                        for v, r in beside(l, j, m, last):
                            while out_ops and (n >= limit or n >= out_ops[0][0]):
                                out_ops.pop(0)[1]()
                            reduce_item(T, v, r)
                            n += 1
                    if last and due and not any(beside(l, u, m, last) for u in range(j + 1, TURN)
                                                for m in range(groups(l, u))):
                        dve_neg_max(dve, l, T, due.pop())
                    for _, op in out_ops:
                        op()

            turns(dve, l, body)
            for u in outputs_left(l):
                for op in dve_output(dve, l, Turn(l, H // 2 - 1), u):
                    op()

        pool_chain = Chain(sem("pool_link"))

        def pool_link(pool, ins):
            pool_chain.n += 1
            ins.then_inc(pool_chain.sem, 1)
            pool.wait_ge(pool_chain.sem, pool_chain.value())

        def pool_max_parts(pool, l, T, v):
            tt = nc.gpsimd.tensor_tensor
            m, x = max_parts[:, v % 4], neg_max[:, v % 4, :]
            pool.wait_ge(asem(l, "max_known"), T.units(v + 1))
            pool_link(pool, tt(m[:, 0, :], x, zeros[:, :], ALU.add))
            pool_link(pool, tt(rest1[:, :], x, m[:, 0, :], ALU.subtract))
            pool_link(pool, tt(m[:, 1, :], rest1[:, :], zeros[:, :], ALU.add))
            tt(m[:, 2, :], rest1[:, :], m[:, 1, :], ALU.subtract).then_inc(asem(l, "max_parts_ready"), 1)

        PART_LINKS = 3
        PARTS_AHEAD = [whole for whole, _ in BEFORE]

        def pool_attention(pool, l):
            pool.wait_ge(sem(f"v_taken{l}"), NC)

            def values(T, head):
                nc.gpsimd.tensor_copy(VH[head % 2][:, :, 0:HD], V[:, :, T.heads(head), :]).then_inc(asem(l, "values"), 1)

            T0 = Turn(l, 0)
            values(T0, 0)
            for v in range(PARTS_AHEAD[l]):
                pool_max_parts(pool, l, T0, v)

            def body(T, first, last):
                for j in range(TURN):
                    if j % NC == 1 and not (last and slot(j) == 1):
                        if not (first and slot(j) == 0):
                            pool.wait_ge(asem(l, "weighed"), T.groups(slot(j) * STEPS[l] // TC))
                        values(T, slot(j) + 1)
                    for m in range(groups(l, j)):
                        for v, r in beside(l, j, m, last):
                            if is_last_item(l, v, r):
                                pool_max_parts(pool, l, T, v)

            turns(pool, l, body, pool_chain, TURN * PART_LINKS)

        def load_operands(eng, l, head, s, which):
            for a in range(PARTS):
                rows = slice(a * PARTS * HD, (a + 1) * PARTS * HD)
                if "q" in which:
                    q = bass.AP(QD[l].tensor, head * (HD * N) + a * P * N, [[0, PARTS], [N, HD], [1, N]])
                    eng.dma_start(QS[s][rows, :], q).then_inc(asem(l, "operands"), 16)
                if "k" in which:
                    k = bass.AP(KD[l].tensor, head * (HD * N), [[P * N, PARTS], [N, HD], [1, N]])
                    eng.dma_start(KS[s][rows, :], k).then_inc(asem(l, "operands"), 16)

        def sp_max_rows(sp, l, T, v):
            c = chunk(l, v)
            sp.wait_ge(asem(l, "max_row_copied"), T.units(v + 1))
            dst = QS[slot(v)][SHIFT_ROW:SHIFT_ROW + PARTS, c * C:(c + 1) * C].rearrange("p (t n) -> p t n", t=TC)
            sp.dma_start(dst, max_row[0:PARTS * TC, v % 4, :]).then_inc(asem(l, f"max_shift{v % 2}_"), 16)

        def sp_attention(sp, l):
            sp.wait_ge(sem(f"parts_stored{l}"), 2 * NC * 16)
            load_operands(sp, l, 0, 0, "q")
            for v in range(ROWS_AHEAD[l]):
                sp_max_rows(sp, l, Turn(l, 0), v)

            def body(T, first, last):
                for j in range(TURN):
                    if j % NC == 0 and not (last and slot(j) == 1):
                        if not (first and slot(j) == 0):
                            sp.wait_ge(asem(l, "weighed"), T.groups(slot(j) * STEPS[l] // TC))
                        load_operands(sp, l, T.heads(slot(j) + 1), (slot(j) + 1) % 2, "qk")
                    for _, v in row_events(l, j, last):
                        sp_max_rows(sp, l, T, v)
                    if l == 0 and first:
                        for e in range(j * NE // TURN, (j + 1) * NE // TURN):
                            sp.dma_start(Wg[:, e, :], w_gate[e]).then_inc(sem("wgu_loaded"), 16)
                            sp.dma_start(Wu[:, e, :], w_up[e]).then_inc(sem("wgu_loaded"), 16)

            turns(sp, l, body)

        def staggered(eng, stages, apart):
            for step in range(stages[-1][0] + apart * (NC - 1) + 1):
                for k, part in reversed(stages):
                    c, off = divmod(step - k, apart)
                    if off == 0 and 0 <= c < NC:
                        part(eng, c)

        moments_of = {}

        def dve_chunk_moments(dve, src, what, c):
            dve_moments(dve, lambda t: tile_of(src, c, t), c)
            std_chain.n += 1
            moments_of[what, c] = std_chain.n

        def dve_normalise(dve, dst, src, what, c):
            dve_inverse_std(dve, c, moments_of[what, c])
            for t in range(TC):
                ins = dve_scale(tile_of(dst, c, t), tile_of(src, c, t), c, t)
            return ins

        def dve_residual(dve, what, c):
            dve_link(dve, dve_normalise(dve, XN, XN, what, c))
            dve_link(dve, nc.vector.tensor_tensor(chunk_of(X, c), chunk_of(X, c), chunk_of(XN, c), ALU.add))

        def pe_transposes(src, b):
            for t in range(TC):
                ins = nc.tensor.transpose(PS[:, b * C + t * P:b * C + (t + 1) * P], src(t), ident[:, :])
            return ins

        def pe_project(l):
            def part(pe, c):
                pe.wait_ge(asem(l, "o_used"), H * NC)
                if c > 0:
                    pe.wait_ge(sem(f"ot_ready{l}"), c)
                pe_transposes(lambda t: tile_of(ON, c, t), 0).then_inc(sem(f"ot_transposed{l}"), 1)
                pe.wait_ge(sem(f"ot_ready{l}"), c + 1)
                if c > 0:
                    pe.wait_ge(sem(f"y_taken{l}"), c)
                for t in range(TC):
                    ins = nc.tensor.matmul(PS[:, C + t * P:C + (t + 1) * P], XT[:, cols(c, t, P)],
                                           WT[:, W_O[l], :], start=True, stop=True)
                ins.then_inc(sem(f"y_ready{l}"), 1)
            return part

        def act_project(l):
            def part(act, c):
                act.wait_ge(sem(f"ot_transposed{l}"), c + 1)
                nc.scalar.copy(XT[:, cols(c)], bank(0)).then_inc(sem(f"ot_ready{l}"), 1)
            return part

        def dve_project(l):
            def part(dve, c):
                bias = bias_bc[:, 0 if l == 0 else 2, :].unsqueeze(1).broadcast_to((P, TC, P))
                dve.wait_ge(sem(f"y_ready{l}"), c + 1)
                nc.vector.tensor_tensor(chunk_of(XN, c), bank(1).rearrange("p (t n) -> p t n", t=TC), bias,
                                        ALU.add).then_inc(sem(f"y_taken{l}"), 1)
                dve.wait_ge(sem(f"y_taken{l}"), c + 1)
                dve_chunk_moments(dve, XN, "project", c)
            return part

        def dve_projected(dve, c):
            dve_residual(dve, "project", c)
            dve_chunk_moments(dve, X, "mixture", c)

        def dve_mixture_input(name):
            def part(dve, c):
                dve_normalise(dve, XN, X, "mixture", c).then_inc(sem(name), 1)
            return part

        def pe_scores(pe, c):
            pe.wait_ge(sem("pick_xn"), c + 1)
            if c > 0:
                pe.wait_ge(sem("pick_xt"), c)
            pe_transposes(lambda t: tile_of(XN, c, t), 2).then_inc(sem("pick_transposed"), 1)
            pe.wait_ge(sem("pick_xt"), c + 1)
            if c > 0:
                pe.wait_ge(sem("pick_hit"), c)
            for t in range(TC):
                ins = nc.tensor.matmul(PS[:, 3 * C + t * NE:3 * C + (t + 1) * NE], XT[:, cols(c, t, P)], gateT[:, :],
                                       start=True, stop=True)
            ins.then_inc(sem("pick_scores"), 1)

        def act_scores(act, c):
            act.wait_ge(sem("pick_transposed"), c + 1)
            nc.scalar.copy(XT[:, cols(c)], bank(2)).then_inc(sem("pick_xt"), 1)

        def dve_scores(dve, c):
            dve.wait_ge(sem("pick_scores"), c + 1)
            s = bank(3)[:, 0:TC * NE].rearrange("p (t e) -> p t e", t=TC)

            def bc(v):
                return v.unsqueeze(2).broadcast_to((P, TC, NE))

            dve_link(dve, nc.vector.tensor_reduce(sc_max[:, :], s, AX.X, ALU.max))
            dve_link(dve, nc.vector.tensor_tensor(sc_hit[:, :, :], s, bc(sc_max[:, :]), ALU.is_equal))
            nc.vector.tensor_tensor(sc_hit[:, :, :], sc_hit[:, :, :], tie[:, :, :], ALU.mult)\
                .then_inc(sem("pick_hit"), 1)
            dve.wait_ge(sem("pick_hit"), c + 1)
            dve_link(dve, nc.vector.tensor_reduce(sc_max[:, :], sc_hit[:, :, :], AX.X, ALU.max))
            nc.vector.tensor_tensor(onehot[:, c, :, :], sc_hit[:, :, :], bc(sc_max[:, :]), ALU.is_equal)\
                .then_inc(sem("pick_onehot"), 1)

        def pe_experts(pe, c):
            for t in range(TC):
                n = c * TC + t
                if n >= 2:
                    pe.wait_ge(sem("pick_masked"), n - 1)
                for i in range(2):
                    w = WT[:, W_E + 4 * i:W_E + 4 * (i + 1), :].rearrange("p e f -> p (e f)")
                    ins = nc.tensor.matmul(bank(4 + 2 * (t % 2) + i), XT[:, cols(c, t, P)], w, start=True, stop=True)
                ins.then_inc(sem("pick_experts"), 1)

        def act_experts(act, c):
            act.wait_ge(sem("pick_onehot"), c + 1)
            for t in range(TC):
                n = c * TC + t
                if n >= 4:
                    act.wait_ge(sem("pick_summed"), n - 3)
                act.wait_ge(sem("pick_experts"), n + 1)
                b = bank(4 + 2 * (t % 2), 2).rearrange("p (e f) -> p e f", e=NE)
                for e in range(NE):
                    ins = nc.scalar.activation(picked[t][:, e, :], b[:, e, :], ACT.Copy, scale=onehot[:, c, t, e:e + 1])
                ins.then_inc(sem("pick_masked"), 1)

        def dve_experts(dve, c):
            for t in range(TC):
                dve.wait_ge(sem("pick_masked"), c * TC + (t + 1))
                nc.vector.tensor_reduce(pick_sum[:, :], picked[t].rearrange("p e f -> p f e"), AX.X, ALU.add)\
                    .then_inc(sem("pick_summed"), 1)
                dve.wait_ge(sem("pick_summed"), c * TC + (t + 1))
                x = tile_of(XN, c, t)
                dve_link(dve, nc.vector.tensor_tensor(x, x, pick_sum[:, :], ALU.add))
            dve_chunk_moments(dve, XN, "experts", c)

        def dve_mixed(dve, c):
            dve_residual(dve, "experts", c)
            dve_chunk_moments(dve, X, "front", c)

        def dve_front_moments(dve, c):
            dve.wait_ge(sem(f"x_loaded{c}"), 16)
            dve_chunk_moments(dve, X, "front", c)

        def dve_front_input(l):
            def part(dve, c):
                dve_normalise(dve, XN, X, "front", c).then_inc(sem(f"xn_ready{l}"), 1)
            return part

        V_BANK = [3, 1]

        def pe_front(l):
            def part(pe, c):
                v_at = V_BANK[l] * C
                pe.wait_ge(sem(f"xn_ready{l}"), c + 1)
                if c > 0:
                    pe.wait_ge(sem(f"qk_biased{l}"), c * 2)
                pe_transposes(lambda t: tile_of(XN, c, t), 0).then_inc(sem(f"x_transposed{l}"), 1)
                pe.wait_ge(sem(f"xt_ready{l}"), c + 1)
                if c > 0 and l == 1:
                    pe.wait_ge(sem(f"v_taken{l}"), c)
                for i, w in ((0, W_Q[l]), (1, W_K[l])):
                    nc.tensor.matmul(bank(1 - i), WT[:, w, :], XT[:, cols(c)], start=True, stop=True)\
                        .then_inc(sem(f"qk_ready{l}"), 1)
                if l == 1:
                    pe.wait_ge(sem(f"qk_biased{l}"), c * 2 + 1)
                elif c > 0:
                    pe.wait_ge(sem(f"v_taken{l}"), c)
                for t in range(TC):
                    ins = nc.tensor.matmul(PS[:, v_at + t * P:v_at + (t + 1) * P], XT[:, cols(c, t, P)],
                                           WT[:, W_V[l], :], start=True, stop=True)
                ins.then_inc(sem(f"v_ready{l}"), 1)
            return part

        def values_of(c):
            return V[:, c * TC:(c + 1) * TC, :, 0:HD]

        def v_psum(l):
            return bank(V_BANK[l]).rearrange("p (t h d) -> p t h d", t=TC, h=H)

        def act_front(l):
            def part(act, c):
                act.wait_ge(sem(f"x_transposed{l}"), c + 1)
                nc.scalar.copy(XT[:, cols(c)], bank(0)).then_inc(sem(f"xt_ready{l}"), 1)
                for i in range(2):
                    act.wait_ge(sem(f"qk_ready{l}"), c * 2 + (i + 1))
                    if c > 0:
                        act.wait_ge(sem(f"parts_ready{l}"), c * 2 - 1 + i)
                    if l == 0:
                        ins = nc.scalar.copy(QF[i], bank(1 - i))
                    else:
                        ins = nc.scalar.activation(QF[i], bank(1 - i), ACT.Identity, bias=bias_qk[:, i:i + 1])
                    ins.then_inc(sem(f"qk_biased{l}"), 1)
                if l == 0:
                    act.wait_ge(sem(f"v_ready{l}"), c + 1)
                    nc.scalar.copy(values_of(c), v_psum(l)).then_inc(sem(f"v_taken{l}"), 1)
            return part

        def dve_front(l):
            def part(dve, c):
                p = [[parts[:, a, cols(c)] for a in range(PARTS)] for parts in (QP, KP)]
                for i in range(2):
                    dve.wait_ge(sem(f"qk_biased{l}"), c * 2 + (i + 1))
                    nc.vector.tensor_copy(p[i][0], QF[i]).then_inc(sem(f"cut{l}"), 1)
                for i in range(2):
                    dve.wait_ge(sem(f"cut{l}"), c * 6 + (i + 1))
                    nc.vector.tensor_tensor(QR[i], QF[i], p[i][0], ALU.subtract).then_inc(sem(f"cut{l}"), 1)
                for i in range(2):
                    dve.wait_ge(sem(f"cut{l}"), c * 6 + (i + 3))
                    nc.vector.tensor_copy(p[i][1], QR[i]).then_inc(sem(f"cut{l}"), 1)
                for i in range(2):
                    dve.wait_ge(sem(f"cut{l}"), c * 6 + (i + 5))
                    nc.vector.tensor_tensor(p[i][2], QR[i], p[i][1], ALU.subtract).then_inc(sem(f"parts_ready{l}"), 1)
                if l == 1:
                    dve.wait_ge(sem(f"v_ready{l}"), c + 1)
                    b = bias_bc[:, 1, :].rearrange("p (h d) -> p h d", h=H).unsqueeze(1).broadcast_to((P, TC, H, HD))
                    nc.vector.tensor_tensor(values_of(c), v_psum(l), b, ALU.add).then_inc(sem(f"v_taken{l}"), 1)
            return part

        def sp_front(sp, l):
            for c in range(NC):
                for i, (parts, dst) in enumerate(((QP, QD[l]), (KP, KD[l]))):
                    sp.wait_ge(sem(f"parts_ready{l}"), c * 2 + (i + 1))
                    sp.dma_start(dst[:, :, cols(c)].rearrange("a p n -> p a n"), parts[:, :, cols(c)])\
                        .then_inc(sem(f"parts_stored{l}"), 16)

        DVE_FIRST = [(0, dve_front_moments), (1, dve_front_input(0)), (3, dve_front(0))]
        ACT_FIRST = [(0, act_std), (2, act_front(0))]
        PE_FIRST = [(2, pe_front(0))]

        PE_MIDDLE = [(0, pe_project(0)), (4, pe_scores), (6, pe_experts), (10, pe_front(1))]
        ACT_MIDDLE = [(0, act_project(0)), (1, act_std), (2, act_std), (4, act_scores), (6, act_experts),
                      (7, act_std), (8, act_std), (10, act_front(1))]
        DVE_MIDDLE = [(1, dve_project(0)), (2, dve_projected), (3, dve_mixture_input("pick_xn")), (5, dve_scores),
                      (7, dve_experts), (8, dve_mixed), (9, dve_front_input(1)), (11, dve_front(1))]

        def pe_logits(pe, c):
            pe.wait_ge(sem("mix_xn"), c + 1)
            if c > 0:
                pe.wait_ge(sem("mix_xt"), c)
            pe_transposes(lambda t: tile_of(XN, c, t), 2).then_inc(sem("mix_transposed"), 1)
            pe.wait_ge(sem("mix_xt"), c + 1)
            for t in range(TC):
                at = 3 * C + (c * TC + t) * 2 * NE
                ins = nc.tensor.matmul(PS[:, at:at + 2 * NE], XT[:, cols(c, t, P)],
                                       rgw[:, :, :].rearrange("p k e -> p (k e)"), start=True, stop=True)
            ins.then_inc(sem("mix_logits"), 1)

        def act_logits(act, c):
            act.wait_ge(sem("mix_transposed"), c + 1)
            nc.scalar.copy(XT[:, cols(c)], bank(2)).then_inc(sem("mix_xt"), 1)

        PE_LAST = [(0, pe_project(1)), (5, pe_logits)]
        ACT_LAST = [(0, act_project(1)), (2, act_std), (3, act_std), (5, act_logits)]
        DVE_LAST = [(2, dve_project(1)), (3, dve_projected), (4, dve_mixture_input("mix_xn"))]

        def after_first(eng, chains, per, body):
            body(0, True)
            for ch, p in zip(chains, per):
                ch.n -= p
            with eng.Fori(1, NC) as c:
                for ch, p in zip(chains, per):
                    ch.enter(c, p)
                body(c, False)
            for ch in chains:
                ch.leave(NC)

        def dve_mix(dve):
            dve.sem_inc(sem("mix_got"), 1)
            dve.wait_ge(sem("mix_logits"), NC)

            def bc(v):
                return v.unsqueeze(3).broadcast_to((P, NT, 2, NE))

            lg = bank(3)[:, 0:NT * 2 * NE].rearrange("p (t k e) -> p t k e", t=NT, k=2)
            dve_link(dve, nc.vector.tensor_reduce(lred[:, :, :], lg, AX.X, ALU.max))
            nc.vector.tensor_tensor(logit[:, :, :, :], lg, bc(lred[:, :, :]), ALU.subtract).then_inc(sem("mix_shifted"), 1)
            dve.wait_ge(sem("mix_exp"), 2)
            dve_link(dve, nc.vector.tensor_reduce(lred[:, :, :], expo[:, :, :, :], AX.X, ALU.add))
            dve_link(dve, nc.vector.reciprocal(linv[:, :, :], lred[:, :, :]))
            dve_link(dve, nc.vector.tensor_tensor(logit[:, :, :, :], expo[:, :, :, :], bc(linv[:, :, :]), ALU.mult))
            dve_link(dve, nc.vector.tensor_tensor(cw[:, :, :], logit[:, :, 0, :], logit[:, :, 1, :], ALU.mult))
            dve_link(dve, nc.vector.tensor_reduce(lred[:, :, 0], cw[:, :, :], AX.X, ALU.add))
            dve_link(dve, nc.vector.tensor_scalar(linv[:, :, 0], lred[:, :, 0], 1e-9, None, ALU.add))
            dve_link(dve, nc.vector.reciprocal(lred[:, :, 1], linv[:, :, 0]))
            nc.vector.tensor_tensor(cw_by_expert.rearrange("p e t -> p t e"), cw[:, :, :],
                                    lred[:, :, 1].unsqueeze(2).broadcast_to((P, NT, NE)), ALU.mult)\
                .then_inc(sem("mix_cw"), 1)
            after_first(dve, [link_chain, var_chain, std_chain], [4, 1, 1], lambda c, first: dve_mix_chunk(dve, c, first))
            for step in mix_post(dve, NC - 1):
                step()

        CW_HALF = NE // 2
        POST_AT = [3, 6, 8]
        STD_AT = 5

        def mix_post(dve, c):
            def take():
                dve.wait_ge(sem("mix_back"), c + 1)
                nc.vector.tensor_copy(chunk_of(XN, c), bank(0).rearrange("p (t n) -> p t n", t=TC))\
                    .then_inc(sem("mix_got"), 1)
                dve.wait_ge(sem("mix_got"), c + 2)
                dve_moments(dve, lambda t: tile_of(XN, c, t), 0)

            def scale():
                dve_inverse_std(dve, 0)
                for t in range(TC):
                    ins = dve_scale(tile_of(XN, c, t), tile_of(XN, c, t), 0, t)
                dve_link(dve, ins)

            def residual():
                nc.vector.tensor_tensor(chunk_of(X, c), chunk_of(X, c), chunk_of(XN, c), ALU.add)\
                    .then_inc(sem("x_final"), 1)

            return [take, scale, residual]

        def dve_mix_chunk(dve, c, first):
            def weighted(e):
                if e % CW_HALF == 0:
                    dve.wait_ge(sem(f"cw_loaded{e // CW_HALF}"), c * 16 + 16)
                if not (first and e < 2):
                    dve.wait_ge(sem("mix_u"), c * 32 + 4 * (e - 1))
                nc.vector.tensor_tensor(XC[e % 2], XT[:, cols(c)], CWB[:, e, :], ALU.mult).then_inc(sem("mix_xc"), 1)

            post = [] if first else mix_post(dve, c - 1)
            weighted(0)
            for i in range(32):
                if i % FB == 0 and i // FB + 1 < NE:
                    weighted(i // FB + 1)
                dve.wait_ge(sem("mix_silu"), c * 32 + (i + 1))
                dve.wait_ge(sem("mix_u"), c * 32 + (i + 1))
                if not (first and i < 4):
                    dve.wait_ge(sem("mix_down"), c * 32 + (i - 3))
                nc.vector.tensor_tensor(HB[i % 4], SG[i % 4], bank(4 + i % 2), ALU.mult).then_inc(sem("mix_h"), 1)
                if post and i in POST_AT:
                    post.pop(0)()

        def act_mix(act):
            act.wait_ge(sem("mix_shifted"), 1)
            nc.scalar.activation(expo[:, :, 0, :], logit[:, :, 0, :], ACT.Exp).then_inc(sem("mix_exp"), 1)
            nc.scalar.activation(expo[:, :, 1, :], logit[:, :, 1, :], ACT.Exp, scale=1.0 / GATE_TEMP)\
                .then_inc(sem("mix_exp"), 1)
            act.wait_ge(sem("cw_transposed"), 1)
            nc.scalar.copy(cwT[:, :], bank(0)[:, 0:P]).then_inc(sem("cw_rows"), 1)

            def body(c, first):
                for i in range(32):
                    act.wait_ge(sem("mix_g"), c * 32 + (i + 1))
                    if not (first and i < 4):
                        act.wait_ge(sem("mix_h"), c * 32 + (i - 3))
                    nc.scalar.activation(SG[i % 4], bank(2 + i % 2), ACT.Silu).then_inc(sem("mix_silu"), 1)
                    if not first and i == STD_AT:
                        act_std(act, 0)
                act.wait_ge(sem("mix_down"), c * 32 + 32)
                if not first:
                    act.wait_ge(sem("mix_back"), c)
                nc.scalar.copy(o_sb[:, 0, :], bank(6)).then_inc(sem("mix_out"), 1)

            after_first(act, act_norms, [1, 1], body)
            act_std(act, 0)

        def pe_mix(pe):
            pe.wait_ge(sem("wgu_loaded"), 2 * NE * 16)
            pe.wait_ge(sem("mix_cw"), 1)
            nc.tensor.transpose(bank(0)[:, 0:P], cw_by_expert[:, :, :].rearrange("p e t -> p (e t)"), ident[:, :])\
                .then_inc(sem("cw_transposed"), 1)
            pe.wait_ge(sem("cw_rows"), 1)

            def back(c):
                pe.wait_ge(sem("mix_out"), c + 1)
                pe.wait_ge(sem("mix_got"), c + 1)
                pe_transposes(lambda t: o_sb[:, 0, t * P:(t + 1) * P], 0).then_inc(sem("mix_back"), 1)

            def down(c, i, first):
                pe.wait_ge(sem("mix_h"), c * 32 + (i + 1))
                if i == 0:
                    if first:
                        pe.wait_ge(sem("wd_loaded"), 16)
                    else:
                        pe.wait_ge(sem("mix_out"), c)
                nc.tensor.matmul(bank(6), Wd[:, i, :], HB[i % 4], start=i == 0, stop=i == 31)\
                    .then_inc(sem("mix_down"), 1)

            def body(c, first):
                for i in range(32):
                    e, f = divmod(i, FB)
                    if not (first and i < 2):
                        pe.wait_ge(sem("mix_silu"), c * 32 + (i - 1))
                    nc.tensor.matmul(bank(2 + i % 2), Wg[:, e, f * P:(f + 1) * P], XT[:, cols(c)], start=True, stop=True)\
                        .then_inc(sem("mix_g"), 1)
                    if f == 0:
                        pe.wait_ge(sem("mix_xc"), c * NE + (e + 1))
                    if not (first and i < 2):
                        pe.wait_ge(sem("mix_h"), c * 32 + (i - 1))
                    nc.tensor.matmul(bank(4 + i % 2), Wu[:, e, f * P:(f + 1) * P], XC[e % 2], start=True, stop=True)\
                        .then_inc(sem("mix_u"), 1)
                    if i >= 1:
                        down(c, i - 1, first)
                    if i == 1 and not first:
                        back(c - 1)
                down(c, 31, first)

            after_first(pe, [], [], body)
            back(NC - 1)

        def sp_mix(sp):
            sp.wait_ge(sem("x_transposed1"), NC)
            sp.wait_ge(asem(1, "o_used"), H * NC)
            sp.dma_start(Wd[:, :, :], w_down.rearrange("e (f p) h -> p (e f) h", p=P)).then_inc(sem("wd_loaded"), 16)
            sp.wait_ge(sem("cw_rows"), 1)
            sp.dma_start(CD.rearrange("e (t n) -> (e t) n", t=NT), cwT[:, :]).then_inc(sem("cw_stored"), 16)
            sp.wait_ge(sem("cw_stored"), 16)
            out_v = out[0].rearrange("(t p) d -> p t d", p=P)

            def store(c):
                sp.wait_ge(sem("x_final"), c + 1)
                sp.dma_start(out_v[:, c * TC:(c + 1) * TC, :], chunk_of(X, c)).then_inc(sem("stored"), 16)


            for c in range(NC):
                for h in range(2):
                    if c > 0:
                        sp.wait_ge(sem("mix_xc"), (c - 1) * NE + (h + 1) * CW_HALF)
                    src = bass.AP(CD.tensor, h * CW_HALF * N + c * C, [[0, P], [N, CW_HALF], [1, C]])
                    sp.dma_start(CWB[:, h * CW_HALF:(h + 1) * CW_HALF, :], src).then_inc(sem(f"cw_loaded{h}"), 16)
                if c > 0:
                    store(c - 1)
            store(NC - 1)
            sp.wait_ge(sem("stored"), NC * 16)

        W_BANK = 3

        def pe_weights(b):
            for i in range(4):
                at = (W_BANK + b) * C + i * P
                ins = nc.tensor.transpose(PS[:, at:at + P], raw[:, 4 * b + i, :], ident[:, :])
            ins.then_inc(sem("w_transposed"), 1)

        def act_weights(act, b):
            act.wait_ge(sem("w_transposed"), b + 1)
            nc.scalar.copy(WT[:, 4 * b:4 * b + 4, :].rearrange("p b c -> p (b c)"), bank(W_BANK + b))\
                .then_inc(sem("w_ready"), 1)

        CONSTS, PADS = 3 + NE, 5
        block = ctx.enter_context(nc.Block())

        @block.sync
        def _(sp):
            x_v = x_in[0].rearrange("(t p) d -> p t d", p=P)
            sp.dma_start(chunk_of(X, 0), x_v[:, 0:TC, :]).then_inc(sem("x_loaded0"), 16)
            sp.dma_start(raw[:, 0:3, :], w_qkv.rearrange("(b p) c -> p b c", p=P)).then_inc(sem("w0_loaded"), 16)
            sp.dma_start(raw[:, 3, :], w_proj).then_inc(sem("w0_loaded"), 16)
            for c in range(1, NC):
                sp.dma_start(chunk_of(X, c), x_v[:, c * TC:(c + 1) * TC, :]).then_inc(sem(f"x_loaded{c}"), 16)
            for i, w in ((4, Wq), (5, Wk), (6, Wv), (7, Wo)):
                sp.dma_start(raw[:, i, :], w).then_inc(sem("w_loaded"), 16)
            sp.dma_start(raw[:, W_E:W_E + NE, :], expert_w.rearrange("e f h -> f e h")).then_inc(sem("w_loaded"), 16)
            sp.dma_start(raw_gate, gate_w).then_inc(sem("w_loaded"), 16)
            for i, b in enumerate((b_proj, bv, bo)):
                sp.dma_start(bias_bc[:, i, :], b.partition_broadcast(P)).then_inc(sem("b_loaded"), 16)
            for i, b in enumerate((bq, bk)):
                sp.dma_start(bias_qk[:, i:i + 1], b.rearrange("(p a) -> p a", a=1)).then_inc(sem("b_loaded"), 16)
            for i, w in enumerate((w_router, w_gating)):
                sp.dma_start(rgw[:, i, :], w).then_inc(sem("b_loaded"), 16)
            sp_front(sp, 0)
            sp.wait_ge(sem("pads"), PADS)
            sp_attention(sp, 0)
            sp_front(sp, 1)
            sp_attention(sp, 1)
            sp_mix(sp)

        @block.gpsimd
        def _(pool):
            nc.gpsimd.memset(ident[:, :], 0.0).then_inc(sem("ident_zeroed"), 1)
            pool.wait_ge(sem("ident_zeroed"), 1)
            nc.gpsimd.affine_select(out=ident[:, :], in_=ident[:, :], compare_op=ALU.not_equal, fill=1.0, base=0,
                                    pattern=[[-1, P]], channel_multiplier=1).then_inc(sem("ident_ready"), 1)
            nc.gpsimd.memset(identb[:, :], 0.0).then_inc(sem("zeroed"), 1)
            nc.gpsimd.memset(mask_nat[:, :], 0.0).then_inc(sem("zeroed"), 1)
            nc.gpsimd.memset(mask_t[:, :], 0.0).then_inc(sem("zeroed"), 1)
            nc.gpsimd.memset(zeros[:, :], 0.0).then_inc(sem("zeroed"), 1)
            pool.wait_ge(sem("zeroed"), 4)
            nc.gpsimd.affine_select(out=identb[:, :], in_=identb[:, :], compare_op=ALU.not_equal, fill=1.0, base=0,
                                    pattern=[[-1, P]], channel_multiplier=1).then_inc(sem("consts"), 1)
            nc.gpsimd.affine_select(out=mask_nat[:, :], in_=mask_nat[:, :], compare_op=ALU.is_ge, fill=MASKED, base=0,
                                    pattern=[[-1, P]], channel_multiplier=1).then_inc(sem("consts"), 1)
            nc.gpsimd.affine_select(out=mask_t[:, :], in_=mask_t[:, :], compare_op=ALU.is_ge, fill=MASKED, base=0,
                                    pattern=[[1, P]], channel_multiplier=-1).then_inc(sem("consts"), 1)
            for e in range(NE):
                nc.gpsimd.memset(tie[:, :, e], float(NE - e)).then_inc(sem("consts"), 1)
            for s in range(2):
                nc.gpsimd.memset(VH[s], 0.0).then_inc(sem("v_zeroed"), 1)
                pool.wait_ge(sem("v_zeroed"), s + 1)
                nc.gpsimd.memset(VH[s][:, :, HD], 1.0).then_inc(sem("pads"), 1)
                nc.gpsimd.memset(QS[s], 0.0).then_inc(sem("pads"), 1)
                nc.gpsimd.memset(KS[s], 0.0).then_inc(sem("ks_zeroed"), 1)
                pool.wait_ge(sem("ks_zeroed"), s + 1)
                nc.gpsimd.memset(KS[s][SHIFT_ROW:P, :], 1.0).then_inc(sem("ks_ones"), 1)
                pool.wait_ge(sem("ks_ones"), s + 1)
            nc.gpsimd.memset(probs_diag[:, :, :, :], 0.0).then_inc(sem("pads"), 1)
            pool.wait_ge(sem("pads"), PADS)
            pool_attention(pool, 0)
            pool_attention(pool, 1)

        @block.scalar
        def _(act):
            act_weights(act, 0)
            staggered(act, ACT_FIRST, 1)
            for b in range(1, 4):
                act_weights(act, b)
            act.wait_ge(sem("w_transposed"), 5)
            nc.scalar.copy(gateT[:, :], bank(W_BANK + 4)[:, 0:NE]).then_inc(sem("w_ready"), 1)
            act.wait_ge(sem("b_loaded"), 7 * 16)
            act.wait_ge(sem("pads"), PADS)
            act_attention(act, 0)
            staggered(act, ACT_MIDDLE, 2)
            act_attention(act, 1)
            staggered(act, ACT_LAST, 1)
            act_mix(act)

        @block.vector
        def _(dve):
            nc.vector.memset(held[:, :], 0.0).then_inc(sem("held_ready"), 1)
            dve.wait_ge(sem("held_ready"), 1)
            staggered(dve, DVE_FIRST, 1)
            dve.wait_ge(sem("b_loaded"), 7 * 16)
            dve.wait_ge(sem("consts"), CONSTS)
            dve_attention(dve, 0)
            staggered(dve, DVE_MIDDLE, 2)
            dve_attention(dve, 1)
            staggered(dve, DVE_LAST, 1)
            dve_mix(dve)

        @block.tensor
        def _(pe):
            pe.wait_ge(sem("ident_ready"), 1)
            pe.wait_ge(sem("w0_loaded"), 2 * 16)
            pe_weights(0)
            pe.wait_ge(sem("w_ready"), 1)
            staggered(pe, PE_FIRST, 1)
            pe.wait_ge(sem("w_loaded"), 6 * 16)
            for b in range(1, 4):
                pe_weights(b)
            nc.tensor.transpose(bank(W_BANK + 4)[:, 0:NE], raw_gate, ident[0:NE, 0:NE]).then_inc(sem("w_transposed"), 1)
            pe.wait_ge(sem("w_ready"), 5)
            pe.wait_ge(sem("b_loaded"), 7 * 16)
            pe.wait_ge(sem("consts"), CONSTS)
            pe.wait_ge(sem("pads"), PADS)
            pe_attention(pe, 0)
            staggered(pe, PE_MIDDLE, 2)
            pe_attention(pe, 1)
            staggered(pe, PE_LAST, 1)
            pe_mix(pe)


INS = ['L0_attn_x', 'L0_attn_w_qkv', 'L0_attn_w_proj', 'L0_attn_b_proj', 'L0_ffn_gate_w', 'L0_ffn_expert_w',
       'L1_attn_Wq', 'L1_attn_bq', 'L1_attn_Wk', 'L1_attn_bk', 'L1_attn_Wv', 'L1_attn_bv', 'L1_attn_Wo', 'L1_attn_bo',
       'L1_ffn_w_router', 'L1_ffn_w_gating', 'L1_ffn_w_gate', 'L1_ffn_w_up', 'L1_ffn_w_down']


def kernel(**inputs):
    import numpy as np
    import concourse.bacc as bacc
    from concourse.bass_utils import run_bass_kernel_spmd

    nc = bacc.Bacc("TRN2", target_bir_lowering=False, num_devices=1)
    arrays, args = {}, []
    for name in INS:
        a = np.ascontiguousarray(inputs[name])
        arrays[f"in_{name}"] = a
        args.append(nc.dram_tensor(f"in_{name}", a.shape, mybir.dt.from_np(a.dtype), kind="ExternalInput").ap())
    out = nc.dram_tensor("out", (1, N, P), FP32, kind="ExternalOutput").ap()
    sandwich(nc, *args, out)
    r = run_bass_kernel_spmd(nc, [arrays], core_ids=[0])
    return r.results[0]["out"]
```
